# Optimizing a Trainium2 kernel written in Bass

```python
import numpy as np
import jax
import jax.numpy as jnp

def _softmax(x, axis=-1):
    return jax.nn.softmax(x, axis=axis)

def _gelu(x):
    return jax.nn.gelu(x, approximate=True)

def _silu(x):
    return jax.nn.silu(x)

def _sigmoid(x):
    return jax.nn.sigmoid(x)

def _layernorm(x, axis=-1, eps=1e-05):
    m = jnp.mean(x, axis=axis, keepdims=True)
    v = jnp.var(x, axis=axis, keepdims=True)
    return (x - m) / jnp.sqrt(v + eps)

def _scatter_add(tgt, idx, src, axis=0):
    return tgt.at[idx].add(src)

def _segment_sum(src, seg, n):
    return jax.ops.segment_sum(src, seg, n)
kernel_name = 'mk_recurrent_d1_jaxref_r2_96d178'

def setup_inputs(seed: int=0):
    np.random.seed(seed)
    _w = jnp.asarray

    def _L0_attn_setup():
        import jax, jax.numpy as jnp
        import numpy as np
        D_MODEL = 512
        HEAD_DIM = 128
        MEMORY_SIZE = 64
        SPARSITY_RATIO = 0.1
        NEG_INF = -1000000000.0

        def _full_attention(x, qkv_w, scale):
            qkv = x @ qkv_w
            q, k, v = jnp.split(qkv, 3, axis=-1)
            scores = jnp.einsum('bsh,bth->bst', q, k) * scale
            probs = jax.nn.softmax(scores, axis=-1)
            return probs @ v

        def _sparse_global_attention(x, qkv_w, scale):
            qkv = x @ qkv_w
            q, k, v = jnp.split(qkv, 3, axis=-1)
            scores = jnp.einsum('bsh,bth->bst', q, k) * scale
            seq_len = x.shape[1]
            k_sparse = max(1, int(seq_len * SPARSITY_RATIO))
            topk_vals, _ = jax.lax.top_k(scores, k_sparse)
            kth = topk_vals[..., -1:]
            masked = jnp.where(scores >= kth, scores, NEG_INF)
            probs = jax.nn.softmax(masked, axis=-1)
            return probs @ v

        def _memory_head(x, memory_bank, memory_proj_w, mem_out_w, mem_out_b):
            x_proj = x @ memory_proj_w
            mem_scores = jnp.einsum('bsh,mh->bsm', x_proj, memory_bank)
            mem_weights = jax.nn.softmax(mem_scores, axis=-1)
            retrieved = jnp.einsum('bsm,mh->bsh', mem_weights, memory_bank)
            combined = jnp.concatenate([x_proj, retrieved], axis=-1)
            return combined @ mem_out_w + mem_out_b

        def _prediction_head(x, pred_in_w, pred_in_b, pred1_w, pred1_b, pred2_w, pred2_b):
            h = x @ pred_in_w + pred_in_b
            h = h @ pred1_w + pred1_b
            h = jax.nn.gelu(h, approximate=False)
            return h @ pred2_w + pred2_b
        key = jax.random.key(seed)
        ks = jax.random.split(key, 16)
        s = lambda fan_in: 1.0 / np.sqrt(fan_in)
        inp = {'x': jax.random.normal(ks[0], (2, 2048, D_MODEL), dtype=jnp.float32), 'local_qkv_w': jax.random.uniform(ks[1], (D_MODEL, 3 * HEAD_DIM), minval=-s(D_MODEL), maxval=s(D_MODEL)), 'sparse_qkv_w': jax.random.uniform(ks[2], (D_MODEL, 3 * HEAD_DIM), minval=-s(D_MODEL), maxval=s(D_MODEL)), 'memory_bank': jax.random.normal(ks[3], (MEMORY_SIZE, HEAD_DIM), dtype=jnp.float32), 'memory_proj_w': jax.random.uniform(ks[4], (D_MODEL, HEAD_DIM), minval=-s(D_MODEL), maxval=s(D_MODEL)), 'mem_out_w': jax.random.uniform(ks[5], (2 * HEAD_DIM, HEAD_DIM), minval=-s(2 * HEAD_DIM), maxval=s(2 * HEAD_DIM)), 'mem_out_b': jax.random.uniform(ks[6], (HEAD_DIM,), minval=-s(2 * HEAD_DIM), maxval=s(2 * HEAD_DIM)), 'pred_in_w': jax.random.uniform(ks[7], (D_MODEL, HEAD_DIM), minval=-s(D_MODEL), maxval=s(D_MODEL)), 'pred_in_b': jax.random.uniform(ks[8], (HEAD_DIM,), minval=-s(D_MODEL), maxval=s(D_MODEL)), 'pred1_w': jax.random.uniform(ks[9], (HEAD_DIM, 2 * HEAD_DIM), minval=-s(HEAD_DIM), maxval=s(HEAD_DIM)), 'pred1_b': jax.random.uniform(ks[10], (2 * HEAD_DIM,), minval=-s(HEAD_DIM), maxval=s(HEAD_DIM)), 'pred2_w': jax.random.uniform(ks[11], (2 * HEAD_DIM, HEAD_DIM), minval=-s(2 * HEAD_DIM), maxval=s(2 * HEAD_DIM)), 'pred2_b': jax.random.uniform(ks[12], (HEAD_DIM,), minval=-s(2 * HEAD_DIM), maxval=s(2 * HEAD_DIM)), 'warboss_w': jax.random.uniform(ks[13], (4 * HEAD_DIM, D_MODEL), minval=-s(4 * HEAD_DIM), maxval=s(4 * HEAD_DIM)), 'warboss_b': jax.random.uniform(ks[14], (D_MODEL,), minval=-s(4 * HEAD_DIM), maxval=s(4 * HEAD_DIM))}
        return inp
    _L0_attn_in = _L0_attn_setup()

    def _L0_ffn_setup():
        import jax, jax.numpy as jnp
        import numpy as np
        B, S, D = (4, 1024, 512)
        N_EXPERTS, EXPERT_SIZE = (16, 128)
        WIDTH = N_EXPERTS * EXPERT_SIZE
        key = jax.random.key(seed)
        k_x, k_w1, k_w2, k_g = jax.random.split(key, 4)
        x = jax.random.normal(k_x, (B, S, D), dtype=jnp.float32)
        w1 = jax.random.normal(k_w1, (D, WIDTH), dtype=jnp.float32) / np.sqrt(D).astype(np.float32)
        b1 = jnp.zeros((WIDTH,), dtype=jnp.float32)
        w2 = jax.random.normal(k_w2, (WIDTH, D), dtype=jnp.float32) / np.sqrt(WIDTH).astype(np.float32)
        b2 = jnp.zeros((D,), dtype=jnp.float32)
        return {'x': x, 'w1': w1, 'b1': b1, 'w2': w2, 'b2': b2}
    _L0_ffn_in = _L0_ffn_setup()
    _d = {'L0_attn_x': _L0_attn_in['x'], 'L0_attn_local_qkv_w': _L0_attn_in['local_qkv_w'], 'L0_attn_sparse_qkv_w': _L0_attn_in['sparse_qkv_w'], 'L0_attn_memory_bank': _L0_attn_in['memory_bank'], 'L0_attn_memory_proj_w': _L0_attn_in['memory_proj_w'], 'L0_attn_mem_out_w': _L0_attn_in['mem_out_w'], 'L0_attn_mem_out_b': _L0_attn_in['mem_out_b'], 'L0_attn_pred_in_w': _L0_attn_in['pred_in_w'], 'L0_attn_pred_in_b': _L0_attn_in['pred_in_b'], 'L0_attn_pred1_w': _L0_attn_in['pred1_w'], 'L0_attn_pred1_b': _L0_attn_in['pred1_b'], 'L0_attn_pred2_w': _L0_attn_in['pred2_w'], 'L0_attn_pred2_b': _L0_attn_in['pred2_b'], 'L0_attn_warboss_w': _L0_attn_in['warboss_w'], 'L0_attn_warboss_b': _L0_attn_in['warboss_b'], 'L0_ffn_w1': _L0_ffn_in['w1'], 'L0_ffn_b1': _L0_ffn_in['b1'], 'L0_ffn_w2': _L0_ffn_in['w2'], 'L0_ffn_b2': _L0_ffn_in['b2']}
    _x0 = _d['L0_attn_x']
    _d['L0_attn_x'] = jax.random.normal(jax.random.fold_in(jax.random.key(seed), 1), (8, 1024, 512), dtype=_x0.dtype)
    del _x0
    return _d

def reference(L0_attn_x, L0_attn_local_qkv_w, L0_attn_sparse_qkv_w, L0_attn_memory_bank, L0_attn_memory_proj_w, L0_attn_mem_out_w, L0_attn_mem_out_b, L0_attn_pred_in_w, L0_attn_pred_in_b, L0_attn_pred1_w, L0_attn_pred1_b, L0_attn_pred2_w, L0_attn_pred2_b, L0_attn_warboss_w, L0_attn_warboss_b, L0_ffn_w1, L0_ffn_b1, L0_ffn_w2, L0_ffn_b2):

    def _L0_attn_ref(x, local_qkv_w, sparse_qkv_w, memory_bank, memory_proj_w, mem_out_w, mem_out_b, pred_in_w, pred_in_b, pred1_w, pred1_b, pred2_w, pred2_b, warboss_w, warboss_b):
        import jax, jax.numpy as jnp
        import numpy as np
        D_MODEL = 512
        HEAD_DIM = 128
        MEMORY_SIZE = 64
        SPARSITY_RATIO = 0.1
        NEG_INF = -1000000000.0

        def _full_attention(x, qkv_w, scale):
            qkv = x @ qkv_w
            q, k, v = jnp.split(qkv, 3, axis=-1)
            scores = jnp.einsum('bsh,bth->bst', q, k) * scale
            probs = jax.nn.softmax(scores, axis=-1)
            return probs @ v

        def _sparse_global_attention(x, qkv_w, scale):
            qkv = x @ qkv_w
            q, k, v = jnp.split(qkv, 3, axis=-1)
            scores = jnp.einsum('bsh,bth->bst', q, k) * scale
            seq_len = x.shape[1]
            k_sparse = max(1, int(seq_len * SPARSITY_RATIO))
            topk_vals, _ = jax.lax.top_k(scores, k_sparse)
            kth = topk_vals[..., -1:]
            masked = jnp.where(scores >= kth, scores, NEG_INF)
            probs = jax.nn.softmax(masked, axis=-1)
            return probs @ v

        def _memory_head(x, memory_bank, memory_proj_w, mem_out_w, mem_out_b):
            x_proj = x @ memory_proj_w
            mem_scores = jnp.einsum('bsh,mh->bsm', x_proj, memory_bank)
            mem_weights = jax.nn.softmax(mem_scores, axis=-1)
            retrieved = jnp.einsum('bsm,mh->bsh', mem_weights, memory_bank)
            combined = jnp.concatenate([x_proj, retrieved], axis=-1)
            return combined @ mem_out_w + mem_out_b

        def _prediction_head(x, pred_in_w, pred_in_b, pred1_w, pred1_b, pred2_w, pred2_b):
            h = x @ pred_in_w + pred_in_b
            h = h @ pred1_w + pred1_b
            h = jax.nn.gelu(h, approximate=False)
            return h @ pred2_w + pred2_b
        scale = HEAD_DIM ** (-0.5)
        local_out = _full_attention(x, local_qkv_w, scale)
        sparse_out = _sparse_global_attention(x, sparse_qkv_w, scale)
        mem_out = _memory_head(x, memory_bank, memory_proj_w, mem_out_w, mem_out_b)
        pred_out = _prediction_head(x, pred_in_w, pred_in_b, pred1_w, pred1_b, pred2_w, pred2_b)
        combined = jnp.concatenate([local_out, sparse_out, mem_out, pred_out], axis=-1)
        return combined @ warboss_w + warboss_b

    def _L0_ffn_ref(x, w1, b1, w2, b2):
        import jax, jax.numpy as jnp
        import numpy as np
        B, S, D = (4, 1024, 512)
        N_EXPERTS, EXPERT_SIZE = (16, 128)
        WIDTH = N_EXPERTS * EXPERT_SIZE
        h = jax.nn.relu(jnp.einsum('bsd,dw->bsw', x, w1) + b1)
        return jnp.einsum('bsw,wd->bsd', h, w2) + b2
    x = L0_attn_x
    xn = _layernorm(x, axis=-1)
    s = _L0_attn_ref(xn, L0_attn_local_qkv_w, L0_attn_sparse_qkv_w, L0_attn_memory_bank, L0_attn_memory_proj_w, L0_attn_mem_out_w, L0_attn_mem_out_b, L0_attn_pred_in_w, L0_attn_pred_in_b, L0_attn_pred1_w, L0_attn_pred1_b, L0_attn_pred2_w, L0_attn_pred2_b, L0_attn_warboss_w, L0_attn_warboss_b)
    g = _silu(_L0_ffn_ref(xn, L0_ffn_w1, L0_ffn_b1, L0_ffn_w2, L0_ffn_b2))
    x = x + s * g
    return x

_drawn_inputs = setup_inputs


def setup_inputs(seed=0):
    import zlib

    import numpy as np

    out = dict(_drawn_inputs(seed))
    spreads = {'L0_ffn_b1': (0.0, 0.8), 'L0_ffn_b2': (0.0, 0.8)}
    factors = {'L0_attn_local_qkv_w': 8.0,
     'L0_attn_sparse_qkv_w': 6.516,
     'L0_attn_mem_out_b': 23.039,
     'L0_attn_pred_in_w': 4.701,
     'L0_attn_pred_in_b': 8.0,
     'L0_attn_pred1_w': 4.743,
     'L0_attn_pred1_b': 8.0,
     'L0_attn_pred2_w': 4.573,
     'L0_attn_pred2_b': 27.7,
     'L0_attn_warboss_b': 5.462,
     'L0_attn_memory_bank': 2.683}
    for name, (base, spread) in spreads.items():
        noise = np.random.default_rng([zlib.crc32(name.encode()), seed]).standard_normal(out[name].shape)
        drawn = base * np.exp(spread * noise) if base else spread * noise
        out[name] = jnp.asarray(drawn.astype(out[name].dtype))
    for name, factor in factors.items():
        out[name] = (out[name] * factor).astype(out[name].dtype)
    return out
```

```python
from contextlib import ExitStack

import concourse.bass as bass
from concourse import mybir

F32 = mybir.dt.float32
F32R = mybir.dt.float32r
I32 = mybir.dt.int32
ALU = mybir.AluOpType
ACT = mybir.ActivationFunctionType
AX_X = mybir.AxisListType.X

P = 128
B, S, D = 8, 1024, 512
HD, MEM = 128, 64
WIDTH = 2048
KT = D // P
HALF = 512
TILES = S // P
HTILES = HALF // P
CH = WIDTH // P
TOPK = max(1, int(S * 0.1))
ROUNDS = (TOPK + 7) // 8
SCALE = HD ** -0.5
EPS = 1e-5
LOWEST = -3.0e38
RSQRT_SEED = float(0x5F3759DF)
NEWTON = 4

MP, PI, QL, QS, KL, KS, VL, VS = range(8)
JOBS = ["mp", "pi", "ql", "ms", "p1a", "p1b", "qs", "wt", "kl", "ret", "p2", "ks",
        "tr0", "tr1", "tr2", "tr3", "v01", "v23", "mo"]
NJ = len(JOBS)
BANKS = 8
U_KS, U_KL, U_VL, U_VS = 0, 2, 4, 6
T_QL, T_QS, T_MEM, T_PRED = range(4)


def wait_alone(eng, sem, value, passed):
    eng.wait_ge(sem, value)
    eng.sem_inc(passed, 1)


def product(nc, out, w_hi, w_lo, x_hi, x_lo, first, last):
    nc.tensor.matmul(out, w_hi, x_hi, start=first, stop=False)
    nc.tensor.matmul(out, w_hi, x_lo, start=False, stop=False)
    return nc.tensor.matmul(out, w_lo, x_hi, start=False, stop=last)


def build(nc, x, w, out):
    xnT_d = nc.dram_tensor("xnT_scratch", [2 * B, P, KT, HALF], F32)
    kv_d = nc.dram_tensor("kv_scratch", [B, P, 8, HALF], F32)
    tile_d = nc.dram_tensor("tile_scratch", [B * TILES, P, 4, P], F32)
    with ExitStack() as outer:
        def sb(name, shape, dt):
            return outer.enter_context(nc.sbuf_tensor(name, shape, dt))

        ident = sb("ident", [P, P], F32)
        ww_hi = sb("ww_hi", [P, KT, D], F32R)
        ww_lo = sb("ww_lo", [P, KT, D], F32R)
        rows_hi = sb("rows_hi", [P, D], F32R)
        rows_lo = sb("rows_lo", [P, D], F32R)
        pick = sb("pick", [P, 2, P], F32R)
        w2 = sb("w2", [P, CH, D], F32)
        b1 = sb("b1", [P, CH], F32)
        stage1(nc, x, w, xnT_d, kv_d, tile_d, ident, ww_hi, ww_lo, rows_hi, rows_lo, pick, w2, b1)
        stage2(nc, x, w, xnT_d, kv_d, tile_d, ident, ww_hi, ww_lo, rows_hi, rows_lo, pick, w2, b1, out)


def stage1(nc, x, w, xnT_d, kv_d, tile_d, ident, ww_hi, ww_lo, rows_hi, rows_lo, pick, w2, b1):
    XP, PIN, WT, RET = range(4)
    LO = ["xp", "pin", "gelu", "wt", "ret"]
    KV_SLOT = {"ks": 0, "kl": 1}
    LN_STEPS = 4 + 4 * NEWTON
    PER = 2 * NJ
    SM_LOADS = 9
    WQ_LOADS = 8

    with ExitStack() as ctx:
        def sb(name, shape, dt):
            return ctx.enter_context(nc.sbuf_tensor(name, shape, dt))

        def sem(name):
            return ctx.enter_context(nc.semaphore(name))

        wp_hi = sb("wp_hi", [P, KT, 8 * P], F32R)
        wp_lo = sb("wp_lo", [P, KT, 8 * P], F32R)
        wload = sb("wload", [P, 8 * P], F32)
        sm = sb("sm", [P, 7, P], F32)
        sm_hi = sb("sm_hi", [P, 7, P], F32R)
        sm_lo = sb("sm_lo", [P, 7, P], F32R)
        bkT = sb("bkT", [P, MEM], F32)
        bkT_hi = sb("bkT_hi", [P, MEM], F32R)
        bkT_lo = sb("bkT_lo", [P, MEM], F32R)
        pick32 = sb("pick32", [P, 2, P], F32)
        rows32 = sb("rows32", [P, D], F32)
        b_pi = sb("b_pi", [P, 1], F32)
        b_p1 = sb("b_p1", [P, 2], F32)
        b_p2 = sb("b_p2", [P, 1], F32)
        b_mo = sb("b_mo", [P, 1], F32)
        xin = sb("xin1", [P, HTILES, D], F32)
        stats = sb("stats", [P, HTILES, 6], F32)
        mv = sb("mv", [P, HTILES, 2], F32)
        var = sb("var", [P, HTILES], F32)
        rstd = sb("rstd", [P, HTILES], F32)
        nt = sb("nt", [P, HTILES], F32)
        xn = sb("xn", [P, HTILES, D], F32)
        xnT = sb("xnT1", [P, KT, HALF], F32)
        xnT_hi = sb("xnT1_hi", [P, 2, KT, HALF], F32R)
        xnT_lo = sb("xnT1_lo", [P, 2, KT, HALF], F32R)
        act32 = sb("act32", [P, 2, HALF], F32)
        act_hi = sb("act_hi", [P, 4, HALF], F32R)
        act_lo = sb("act_lo", [P, 4, HALF], F32R)
        gelu = wload[:, :].rearrange("p (c n) -> p c n", c=2)
        gelu_hi = sb("gelu_hi", [P, 2, HALF], F32R)
        gelu_lo = sb("gelu_lo", [P, 2, HALF], F32R)
        nmx = sb("nmx", [P, HTILES], F32)
        esum = sb("esum", [P, HTILES], F32)
        einv = sb("einv", [P, HTILES], F32)
        we = sb("we", [P, HTILES, MEM], F32)
        tiles_out = sb("tiles_out", [P, HTILES, 4, P], F32)
        kv_out = sb("kv_out", [P, 4, HALF], F32)
        ps = ctx.enter_context(nc.psum_tensor("ps1", [P, BANKS, 512], F32))

        w_in = [sem(f"w_in{k}") for k in range(2 * KT)]
        sm_in = sem("sm_in")
        rows_in = sem("rows_in")
        w2_in = sem("w2_in")
        consts = sem("consts")
        prep = sem("prep")
        w_split = sem("w_split")
        sm_split = sem("sm_split")
        bkT_ps = sem("bkT_ps")
        bkT_out = sem("bkT_out")
        bkT_split = sem("bkT_split")
        x_in = sem("x_in")
        ln_step = sem("ln_step")
        xn_ready = sem("xn_ready")
        job_done = sem("job_done")
        bank_read = sem("bank_read")
        lo_ready = sem("lo_ready")
        ghi_ready = sem("ghi_ready")
        xlo_ready = sem("xlo_ready")
        max_ready = sem("max_ready")
        inv_ready = sem("inv_ready")
        wn_ready = sem("wn_ready")
        tiles_st = sem("tiles_st")
        kv_st = sem("kv_st")
        xnT_st = sem("xnT_st")
        sp_passed, pe_passed = sem("sp1_passed"), sem("pe_passed")

        def done(n, name):
            return KT + n * NJ + JOBS.index(name) + 1

        def bank(hh, name):
            return (KT + hh * NJ + JOBS.index(name)) % BANKS

        def bank_free(b, hh, name):
            p = hh * NJ + JOBS.index(name)
            own = [q for q in range(-KT, p) if (q - p) % BANKS == 0]
            if isinstance(b, int):
                return KT + own[-1] + 1 if own else None
            near = max(q for q in range(p - BANKS - PER, p) if
                       (q >= 0 and (q - p) % BANKS == 0) or (q < 0 and (q + PER - p) % BANKS == 0))
            return KT + b * PER + near + 1

        def lo(n, name):
            return n * len(LO) + LO.index(name) + 1

        def first(n):
            return isinstance(n, int) and n == 0

        with nc.Block() as block:
            @block.sync
            def _(sp):
                lq, sq = w["local_qkv_w"], w["sparse_qkv_w"]
                sp.dma_start(xin[:, :, :], x[0, 0:HALF, :].rearrange("(t p) d -> p t d", p=P)).then_inc(x_in, 16)
                for k in range(2 * KT):
                    if k >= 1:
                        sp.wait_ge(w_split, k)
                    r = slice((k % KT) * P, (k % KT + 1) * P)
                    if k < KT:
                        pieces = [w["memory_proj_w"][r, :], w["pred_in_w"][r, :], lq[r, 0:P], sq[r, 0:P],
                                  lq[r, P:2 * P], sq[r, P:2 * P], lq[r, 2 * P:3 * P], sq[r, 2 * P:3 * P]]
                        for m, piece in enumerate(pieces):
                            sp.dma_start(wload[:, m * P:(m + 1) * P], piece).then_inc(w_in[k], 16)
                    else:
                        sp.dma_start(wload[:, 0:D], w["warboss_w"][r, :]).then_inc(w_in[k], 16)
                sp.dma_start(w2[:, :, :], w["w2"].rearrange("(c p) n -> p c n", p=P)).then_inc(w2_in, 16)

                def steps(b):
                    for hh in range(2):
                        n = 2 * b + hh
                        nb, nh = (b, 1) if hh == 0 else ((b + 1) & (B - 1), 0)
                        wait_alone(sp, xn_ready, n + 1, sp_passed)
                        sp.dma_start(xin[:, :, :],
                                     x[bass.ds(nb, 1), nh * HALF:(nh + 1) * HALF, :]
                                     .rearrange("a (t p) d -> p (a t) d", p=P)).then_inc(x_in, 16)
                        sp.wait_ge(bank_read, KT if first(n) else done(n - 1, "tr3"))
                        sp.dma_start(xnT_d[bass.ds(n, 1), :, :, :].rearrange("a p k n -> p (a k) n"),
                                     xnT[:, :, :]).then_inc(xnT_st, 16)
                        wait_alone(sp, bank_read, done(n, "v23"), sp_passed)
                        sp.dma_start(kv_d[bass.ds(b, 1), :, :, :]
                                     .rearrange("a p (u h) n -> p (a u) h n", h=2)[:, :, hh, :],
                                     kv_out[:, :, :]).then_inc(kv_st, 16)
                        sp.wait_ge(bank_read, done(n, "mo"))
                        sp.dma_start(tile_d[bass.ds(n * HTILES, HTILES), :, :, :].rearrange("t p s n -> p t (s n)"),
                                     tiles_out[:, :, :, :].rearrange("p t s n -> p t (s n)")).then_inc(tiles_st, 16)

                steps(0)
                with sp.Fori(1, B) as b:
                    steps(b)
                sp.wait_ge(xnT_st, 16 * 2 * B)
                sp.wait_ge(kv_st, 16 * 2 * B)
                sp.wait_ge(tiles_st, 16 * 2 * B)
                sp.wait_ge(w2_in, 16)

            @block.gpsimd
            def _(pool):
                pool.memset(rows32[:, :], 0.0).then_inc(consts, 1)
                pool.wait_ge(consts, 1)
                pool.memset(sm[MEM:P, 6, :], 0.0).then_inc(consts, 1)
                pool.wait_ge(consts, 2)
                pool.memset(ident[:, :], 0.0).then_inc(consts, 1)
                pool.wait_ge(consts, 3)
                pool.memset(pick32[:, :, :], 1.0).then_inc(consts, 1)
                pool.wait_ge(consts, 4)
                pool.affine_select(out=ident[:, :], in_=ident[:, :], compare_op=ALU.not_equal, fill=1.0,
                                   base=0, pattern=[[-1, P]], channel_multiplier=1).then_inc(consts, 1)
                pool.wait_ge(consts, 5)
                pool.affine_select(out=pick32[:, :, :], in_=pick32[:, :, :], compare_op=ALU.is_equal, fill=0.0,
                                   base=0, pattern=[[-1, 2], [0, P]], channel_multiplier=1).then_inc(consts, 1)

            @block.scalar
            def _(act):
                def column(name):
                    return w[name].rearrange("(p a) -> p a", a=1)

                act.dma_start(sm[:, 0:2, :], w["mem_out_w"].rearrange("(k p) n -> p k n", p=P)).then_inc(sm_in, 16)
                act.dma_start(sm[:, 2:4, :], w["pred1_w"].rearrange("p (k n) -> p k n", k=2)).then_inc(sm_in, 16)
                act.dma_start(sm[:, 4:6, :], w["pred2_w"].rearrange("(k p) n -> p k n", p=P)).then_inc(sm_in, 16)
                act.dma_start(sm[0:MEM, 6, :], w["memory_bank"]).then_inc(sm_in, 16)
                act.dma_start(b_pi[:, :], column("pred_in_b")).then_inc(sm_in, 16)
                act.dma_start(b_p2[:, :], column("pred2_b")).then_inc(sm_in, 16)
                act.dma_start(b_mo[:, :], column("mem_out_b")).then_inc(sm_in, 16)
                with nc.allow_non_contiguous_dma(reason="biases by column"):
                    act.dma_start(b_p1[:, :], w["pred1_b"].rearrange("(k p) -> p k", p=P)).then_inc(sm_in, 16)
                    act.dma_start(b1[:, :], w["b1"].rearrange("(k p) -> p k", p=P)).then_inc(sm_in, 16)
                act.wait_ge(consts, 1)
                act.dma_start(rows32[0:1, :], w["warboss_b"].rearrange("(a n) -> a n", a=1)).then_inc(rows_in, 16)
                act.dma_start(rows32[1:2, :], w["b2"].rearrange("(a n) -> a n", a=1)).then_inc(rows_in, 16)
                act.wait_ge(bkT_ps, 1)
                nc.scalar.activation(bkT[:, :], ps[:, BANKS - 1, 0:MEM], ACT.Copy)
                nc.scalar.activation(bkT_hi[:, :], ps[:, BANKS - 1, 0:MEM], ACT.Copy).then_inc(bkT_out, 1)
                act.wait_ge(sm_in, 16 * SM_LOADS)

                for k in range(KT):
                    act.wait_ge(job_done, k + 1)
                    nc.scalar.activation(xnT[:, k, :], ps[:, k, :], ACT.Copy)
                    nc.scalar.activation(xnT_hi[:, 0, k, :], ps[:, k, :], ACT.Copy).then_inc(bank_read, 1)

                def steps(b):
                    for hh in range(2):
                        n = 2 * b + hh
                        for name in JOBS:
                            src = ps[:, bank(hh, name), :]
                            act.wait_ge(job_done, done(n, name))
                            if name == "mp":
                                nc.scalar.activation(act32[:, XP, :], src, ACT.Copy)
                                last = nc.scalar.activation(act_hi[:, XP, :], src, ACT.Copy)
                            elif name == "pi":
                                nc.scalar.activation(act32[:, PIN, :], src, ACT.Identity, bias=b_pi[:, :])
                                last = nc.scalar.activation(act_hi[:, PIN, :], src, ACT.Identity, bias=b_pi[:, :])
                            elif name == "ret":
                                nc.scalar.activation(act32[:, RET % 2, :], src, ACT.Copy)
                                last = nc.scalar.activation(act_hi[:, RET, :], src, ACT.Copy)
                            elif name == "wt":
                                src = ps[0:MEM, bank(hh, name), :]
                                nc.scalar.activation(act32[0:MEM, WT % 2, :], src, ACT.Copy)
                                last = nc.scalar.activation(act_hi[0:MEM, WT, :], src, ACT.Copy)
                            elif name == "ms":
                                act.wait_ge(max_ready, n + 1)
                                for t in range(HTILES):
                                    last = nc.scalar.activation(we[:, t, :], src[:, t * MEM:(t + 1) * MEM], ACT.Exp,
                                                                bias=nmx[:, t:t + 1], accum_out=esum[:, t:t + 1])
                            elif name in ("p1a", "p1b"):
                                c = int(name == "p1b")
                                if first(n):
                                    act.wait_ge(w_split, 2 * KT)
                                last = nc.scalar.activation(gelu[:, c, :], src, ACT.Gelu, bias=b_p1[:, c:c + 1])
                            elif name in ("ql", "qs", "p2", "mo"):
                                if name == "ql" and not first(n):
                                    act.wait_ge(tiles_st, 16 * n)
                                slot = {"ql": T_QL, "qs": T_QS, "p2": T_PRED, "mo": T_MEM}[name]
                                dst = tiles_out[:, :, slot, :]
                                src = src.rearrange("p (t n) -> p t n", n=P)
                                if name in ("p2", "mo"):
                                    bias = b_p2 if name == "p2" else b_mo
                                    last = nc.scalar.activation(dst, src, ACT.Identity, bias=bias[:, :])
                                else:
                                    last = nc.scalar.activation(dst, src, ACT.Copy)
                            elif name in ("kl", "ks"):
                                if name == "kl" and not first(n):
                                    act.wait_ge(kv_st, 16 * n)
                                last = nc.scalar.activation(kv_out[:, KV_SLOT[name], :], src, ACT.Copy)
                            elif name in ("v01", "v23"):
                                c = 2 * P * int(name == "v23")
                                last = nc.scalar.activation(
                                    kv_out[:, 2:4, c:c + 2 * P].rearrange("p h (t n) -> p t h n", n=P),
                                    src.rearrange("p (t h n) -> p t h n", t=2, h=2), ACT.Copy)
                            else:
                                k = int(name[2])
                                if k == 0:
                                    act.wait_ge(xnT_st, 16 * (n + 1))
                                    act.wait_ge(xlo_ready, KT * (n + 1))
                                nc.scalar.activation(xnT[:, k, :], src, ACT.Copy)
                                last = nc.scalar.activation(xnT_hi[:, 1 - hh, k, :], src, ACT.Copy)
                            last.then_inc(bank_read, 1)

                steps(0)
                with act.Fori(1, B) as b:
                    steps(b)

            @block.vector
            def _(dve):
                def subtract(out, value, hi):
                    return nc.vector.tensor_tensor(out, value, hi.bitcast(F32), ALU.subtract)

                def layer_norm(n):
                    if not first(n):
                        nc.vector.sem_clear(ln_step)
                    dve.wait_ge(x_in, 16 * (n + 1))
                    step = [0]

                    def link(ins):
                        ins.then_inc(ln_step, 1)
                        step[0] = step[0] + 1
                        dve.wait_ge(ln_step, step[0])

                    for t in range(HTILES):
                        last = nc.vector.bn_stats(stats[:, t, :], xin[:, t, :])
                    link(last)
                    for t in range(HTILES):
                        last = nc.vector.bn_aggr(mv[:, t, :], stats[:, t, :])
                    link(last)
                    link(nc.vector.tensor_scalar(var[:, :], mv[:, :, 1], EPS, None, ALU.add))
                    link(nc.vector.tensor_scalar(rstd[:, :].bitcast(I32), var[:, :].bitcast(I32),
                                                 -0.5, RSQRT_SEED, ALU.mult, ALU.add))
                    for _ in range(NEWTON):
                        link(nc.vector.tensor_tensor(nt[:, :], rstd[:, :], rstd[:, :], ALU.mult))
                        link(nc.vector.tensor_tensor(nt[:, :], nt[:, :], var[:, :], ALU.mult))
                        link(nc.vector.tensor_scalar(nt[:, :], nt[:, :], -0.5, 1.5, ALU.mult, ALU.add))
                        link(nc.vector.tensor_tensor(rstd[:, :], rstd[:, :], nt[:, :], ALU.mult))
                    for t in range(HTILES):
                        last = nc.vector.tensor_scalar(xn[:, t, :], xin[:, t, :], mv[:, t, 0:1],
                                                       rstd[:, t:t + 1], ALU.subtract, ALU.mult)
                    last.then_inc(xn_ready, 1)

                layer_norm(0)
                for k in range(2 * KT):
                    dve.wait_ge(w_in[k], 16 * WQ_LOADS if k < KT else 16)
                    hi, lo_, src = ((wp_hi[:, k, :], wp_lo[:, k, :], wload[:, :]) if k < KT else
                                    (ww_hi[:, k - KT, :], ww_lo[:, k - KT, :], wload[:, 0:D]))
                    nc.vector.tensor_copy(hi, src).then_inc(prep, 1)
                    dve.wait_ge(prep, k + 1)
                    subtract(lo_, src, hi).then_inc(w_split, 1)
                    if k == KT - 1:
                        for kk in range(KT):
                            dve.wait_ge(bank_read, kk + 1)
                            subtract(xnT_lo[:, 0, kk, :], xnT[:, kk, :], xnT_hi[:, 0, kk, :]).then_inc(xlo_ready, 1)
                        dve.wait_ge(sm_in, 16 * SM_LOADS)
                        dve.wait_ge(consts, 6)
                        nc.vector.tensor_copy(sm_hi[:, :, :], sm[:, :, :]).then_inc(sm_split, 1)
                        dve.wait_ge(sm_split, 1)
                        subtract(sm_lo[:, :, :], sm[:, :, :], sm_hi[:, :, :]).then_inc(sm_split, 1)
                        dve.wait_ge(bkT_out, 1)
                        subtract(bkT_lo[:, :], bkT[:, :], bkT_hi[:, :]).then_inc(bkT_split, 1)
                dve.wait_ge(rows_in, 32)
                nc.vector.tensor_copy(pick[:, :, :], pick32[:, :, :])
                nc.vector.tensor_copy(rows_hi[:, :], rows32[:, :]).then_inc(prep, 1)
                dve.wait_ge(prep, 2 * KT + 1)
                subtract(rows_lo[:, :], rows32[:, :], rows_hi[:, :])

                def steps(b):
                    for hh in range(2):
                        n = 2 * b + hh
                        for name, slot in (("mp", XP), ("pi", PIN)):
                            dve.wait_ge(bank_read, done(n, name))
                            subtract(act_lo[:, slot, :], act32[:, slot, :], act_hi[:, slot, :]).then_inc(lo_ready, 1)
                        dve.wait_ge(job_done, done(n, "ms"))
                        nc.vector.tensor_reduce(nmx[:, :], ps[:, bank(hh, "ms"), 0:HTILES * MEM]
                                                .rearrange("p (t m) -> p t m", m=MEM), AX_X, ALU.max,
                                                negate=True).then_inc(max_ready, 1)
                        dve.wait_ge(bank_read, done(n, "ms"))
                        nc.vector.reciprocal(einv[:, :], esum[:, :]).then_inc(inv_ready, 1)
                        dve.wait_ge(inv_ready, n + 1)
                        for t in range(HTILES):
                            last = nc.vector.tensor_scalar(we[:, t, :], we[:, t, :], einv[:, t:t + 1], None, ALU.mult)
                        last.then_inc(wn_ready, 1)
                        dve.wait_ge(bank_read, done(n, "p1b"))
                        nc.vector.tensor_copy(gelu_hi[:, :, :], gelu[:, :, :]).then_inc(ghi_ready, 1)
                        dve.wait_ge(ghi_ready, n + 1)
                        subtract(gelu_lo[:, :, :], gelu[:, :, :], gelu_hi[:, :, :]).then_inc(lo_ready, 1)
                        dve.wait_ge(bank_read, done(n, "wt"))
                        subtract(act_lo[0:MEM, WT, :], act32[0:MEM, WT % 2, :], act_hi[0:MEM, WT, :]).then_inc(lo_ready, 1)
                        layer_norm(n + 1)
                        dve.wait_ge(bank_read, done(n, "ret"))
                        subtract(act_lo[:, RET, :], act32[:, RET % 2, :], act_hi[:, RET, :]).then_inc(lo_ready, 1)
                        for k in range(KT):
                            dve.wait_ge(bank_read, done(n, f"tr{k}"))
                            subtract(xnT_lo[:, 1 - hh, k, :], xnT[:, k, :], xnT_hi[:, 1 - hh, k, :])\
                                .then_inc(xlo_ready, 1)

                steps(0)
                with dve.Fori(1, B) as b:
                    steps(b)

            @block.tensor
            def _(pe):
                pe.wait_ge(sm_in, 16 * SM_LOADS)
                pe.wait_ge(consts, 6)
                nc.tensor.transpose(ps[:, BANKS - 1, 0:MEM], sm[0:MEM, 6, :], ident[0:MEM, 0:MEM]).then_inc(bkT_ps, 1)

                def transposes(k, bk):
                    for t in range(HTILES):
                        last = nc.tensor.transpose(ps[:, bk, t * P:(t + 1) * P], xn[:, t, k * P:(k + 1) * P],
                                                   ident[:, :])
                    return last

                pe.wait_ge(xn_ready, 1)
                for k in range(KT):
                    transposes(k, k).then_inc(job_done, 1)
                pe.wait_ge(w_split, KT)
                pe.wait_ge(sm_split, 2)
                pe.wait_ge(bkT_split, 1)

                def steps(b):
                    for hh in range(2):
                        n = 2 * b + hh
                        pe.wait_ge(xlo_ready, KT * (n + 1))
                        for name in JOBS:
                            bk = bank(hh, name)
                            dst = ps[:, bk, :]
                            free = bank_free(b, hh, name)
                            if free is not None:
                                pe.wait_ge(bank_read, free)
                            columns = {"mp": MP, "pi": PI, "ql": QL, "qs": QS, "kl": KL, "ks": KS}
                            if name in columns:
                                c = slice(columns[name] * P, (columns[name] + 1) * P)
                                for k in range(KT):
                                    last = product(nc, dst, wp_hi[:, k, c], wp_lo[:, k, c], xnT_hi[:, hh, k, :],
                                                   xnT_lo[:, hh, k, :], k == 0, k == KT - 1)
                            elif name == "ms":
                                pe.wait_ge(lo_ready, lo(n, "xp"))
                                for t in range(HTILES):
                                    c = slice(t * P, (t + 1) * P)
                                    last = product(nc, dst[:, t * MEM:(t + 1) * MEM], act_hi[:, XP, c],
                                                   act_lo[:, XP, c], bkT_hi[:, :], bkT_lo[:, :], True, True)
                            elif name in ("p1a", "p1b"):
                                c = 2 + int(name == "p1b")
                                pe.wait_ge(lo_ready, lo(n, "pin"))
                                last = product(nc, dst, sm_hi[:, c, :], sm_lo[:, c, :], act_hi[:, PIN, :],
                                               act_lo[:, PIN, :], True, True)
                            elif name == "wt":
                                wait_alone(pe, wn_ready, n + 1, pe_passed)
                                for t in range(HTILES):
                                    last = nc.tensor.transpose(ps[0:MEM, bk, t * P:(t + 1) * P], we[:, t, :],
                                                               ident[:, :])
                            elif name == "ret":
                                pe.wait_ge(lo_ready, lo(n, "wt"))
                                last = product(nc, dst, sm_hi[0:MEM, 6, :], sm_lo[0:MEM, 6, :],
                                               act_hi[0:MEM, WT, :], act_lo[0:MEM, WT, :], True, True)
                            elif name == "p2":
                                pe.wait_ge(lo_ready, lo(n, "gelu"))
                                for c in range(2):
                                    last = product(nc, dst, sm_hi[:, 4 + c, :], sm_lo[:, 4 + c, :],
                                                   gelu_hi[:, c, :], gelu_lo[:, c, :], c == 0, c == 1)
                            elif name == "mo":
                                pe.wait_ge(lo_ready, lo(n, "ret"))
                                for c, slot in enumerate((XP, RET)):
                                    last = product(nc, dst, sm_hi[:, c, :], sm_lo[:, c, :], act_hi[:, slot, :],
                                                   act_lo[:, slot, :], c == 0, c == 1)
                            elif name in ("v01", "v23"):
                                v = slice(VL * P, (VS + 1) * P)
                                for tt in range(2):
                                    t = 2 * int(name == "v23") + tt
                                    c = slice(t * P, (t + 1) * P)
                                    for k in range(KT):
                                        last = product(nc, dst[:, tt * 2 * P:(tt + 1) * 2 * P], xnT_hi[:, hh, k, c],
                                                       xnT_lo[:, hh, k, c], wp_hi[:, k, v], wp_lo[:, k, v],
                                                       k == 0, k == KT - 1)
                            else:
                                if name == "tr0":
                                    pe.wait_ge(xn_ready, n + 2)
                                last = transposes(int(name[2]), bk)
                            last.then_inc(job_done, 1)

                steps(0)
                with pe.Fori(1, B) as b:
                    steps(b)


def stage2(nc, x, w, xnT_d, kv_d, tile_d, ident, ww_hi, ww_lo, rows_hi, rows_lo, pick, w2, b1, out):
    HC = CH // HTILES
    BC = 2 * CH
    GAP = 4

    with ExitStack() as ctx:
        def sb(name, shape, dt):
            return ctx.enter_context(nc.sbuf_tensor(name, shape, dt))

        def sem(name):
            return ctx.enter_context(nc.semaphore(name))

        xnT = sb("xnT", [P, 2, HALF], F32)
        xnT_hi = sb("xnT_hi", [P, KT, HALF], F32R)
        xnT_lo = sb("xnT_lo", [P, KT, HALF], F32R)
        kv = sb("kv", [P, 2, HALF], F32)
        kv_hi = sb("kv_hi", [P, 8, HALF], F32R)
        kv_lo = sb("kv_lo", [P, 8, HALF], F32R)
        tl = sb("tl", [P, 4, P], F32)
        tl_hi = sb("tl_hi", [P, 2, 4, P], F32R)
        tl_lo = sb("tl_lo", [P, 2, 4, P], F32R)
        w1 = sb("w1", [P, 2, KT, P], F32)
        w1_hi = sb("w1_hi", [P, 2, KT, P], F32R)
        w1_lo = sb("w1_lo", [P, 2, KT, P], F32R)
        w2_hi = sb("w2_hi", [P, 2, D], F32R)
        w2_lo = sb("w2_lo", [P, 2, D], F32R)
        h32 = sb("h32", [P, 2, HALF], F32)
        h_hi = sb("h_hi", [P, 2, HALF], F32R)
        h_lo = sb("h_lo", [P, 2, HALF], F32R)
        sc = sb("sc", [P, 2, S], F32)
        work = sb("work", [P, S], F32)
        m8 = sb("m8", [P, 8], F32)
        nms = sb("nms", [P, 2], F32)
        mxl = sb("mxl", [P, 1], F32)
        nml = sb("nml", [P, 1], F32)
        sums = sb("sums", [P, 2], F32)
        inv = sb("inv", [P, 2], F32)
        prob = sb("prob", [P, 2, S], F32)
        pT = sb("pT", [P, 2, 512], F32)
        pT_hi = sb("pT_hi", [P, S], F32R)
        pT_lo = sb("pT_lo", [P, S], F32R)
        at = sb("at", [P, 2, P], F32)
        at_hi = sb("at_hi", [P, 2, P], F32R)
        at_lo = sb("at_lo", [P, 2, P], F32R)
        mixed = sb("mixed", [P, HTILES, D], F32)
        gate = sb("gate", [P, HTILES, D], F32)
        xin = sb("xin", [P, 2, D], F32)
        scores = ctx.enter_context(nc.psum_tensor("scores", [P, S], F32))
        hid = ctx.enter_context(nc.psum_tensor("hid", [P, HALF], F32))
        o = ctx.enter_context(nc.psum_tensor("o", [P, D], F32))
        acc = ctx.enter_context(nc.psum_tensor("acc", [P, HTILES, D], F32))

        w1_in = [sem("w1_in0"), sem("w1_in1")]
        kv_in = [sem("kv_in0"), sem("kv_in1")]
        xn_in = [sem("xn_in0"), sem("xn_in1")]
        xr_in = [sem("xr_in0"), sem("xr_in1")]
        tl_in = sem("tl_in")
        out_st = [sem(f"out_st{t}") for t in range(HTILES)]
        w1_h, w1_l = sem("w1_h"), sem("w1_l")
        w2_h, w2_l = sem("w2_h"), sem("w2_l")
        kv_h, kv_l = sem("kv_h"), sem("kv_l")
        xn_h, xn_l = sem("xn_h"), sem("xn_l")
        tl_h, tl_l = sem("tl_h"), sem("tl_l")
        h_h, h_l = sem("h_h"), sem("h_l")
        pT_h, pT_l = sem("pT_h"), sem("pT_l")
        at_h, at_l = sem("at_h"), sem("at_l")
        f1_done = sem("f1_done")
        f2_done = sem("f2_done")
        ss_done = sem("ss_done")
        sl_done = sem("sl_done")
        tr_done = sem("tr_done")
        pv_done = sem("pv_done")
        mix_done = sem("mix_done")
        sc_ready = sem("sc_ready")
        tanh_ready = sem("tanh_ready")
        mix_ready = sem("mix_ready")
        es_ready = sem("es_ready")
        el_ready = sem("el_ready")
        pr_ready = sem("pr_ready")
        step = sem("step")
        nms_ready = sem("nms_ready")
        nml_step = sem("nml_step")
        nml_ready = sem("nml_ready")
        masked = sem("masked")
        invs_ready = sem("invs_ready")
        invl_ready = sem("invl_ready")
        gate_ready = sem("gate_ready")
        prod_ready = sem("prod_ready")
        fin_ready = sem("fin_ready")

        sp_passed, dve_passed = sem("sp_passed"), sem("dve_passed")

        STEPS = 2 * ROUNDS - 1

        def known_first(v, least):
            return isinstance(v, int) and v < least

        with nc.Block() as block:
            @block.sync
            def _(sp):
                def load_w1(C, c):
                    if not known_first(C, 2):
                        sp.wait_ge(w1_l, C - 1)
                    sp.dma_start(w1[:, c % 2, :, :], w["w1"].rearrange("(k p) n -> p k n", p=P)
                                 [:, :, (c % CH) * P:(c % CH + 1) * P]).then_inc(w1_in[c % 2], 16)

                def load_kv(g, u, b):
                    if not known_first(g, 2):
                        sp.wait_ge(kv_l, g - 1)
                    sp.dma_start(kv[:, u % 2, :], kv_d[bass.ds(b, 1), :, u, :]
                                 .rearrange("a p n -> p (a n)")).then_inc(kv_in[u % 2], 16)

                def load_xn(g, k, h):
                    if not known_first(g, 2):
                        sp.wait_ge(xn_l, g - 1)
                    sp.dma_start(xnT[:, k % 2, :], xnT_d[bass.ds(h, 1), :, k, :]
                                 .rearrange("a p n -> p (a n)")).then_inc(xn_in[k % 2], 16)

                def load_tl(m, src):
                    if not known_first(m, 1):
                        wait_alone(sp, tl_l, m, sp_passed)
                    sp.dma_start(tl[:, :, :], tile_d[bass.ds(src, 1), :, :, :]
                                 .rearrange("a p s n -> p (a s) n")).then_inc(tl_in, 16)

                load_tl(0, 0)
                load_kv(0, U_KS, 0)
                load_kv(1, U_KS + 1, 0)
                load_w1(0, 0)
                load_w1(1, 1)
                for k in range(KT):
                    load_xn(k, k, 0)
                load_w1(2, 2)
                load_w1(3, 3)
                load_kv(2, U_KL, 0)
                load_kv(3, U_KL + 1, 0)

                def load_x(m, b, T):
                    if not known_first(m, 2):
                        wait_alone(sp, fin_ready, m - 1, sp_passed)
                    sp.dma_start(xin[:, T % 2, :], x[bass.ds(b, 1), T * P:(T + 1) * P, :]
                                 .rearrange("a p n -> p (a n)")).then_inc(xr_in[T % 2], 16)

                def store(m, b, T):
                    wait_alone(sp, fin_ready, m + 1, sp_passed)
                    sp.dma_start(out[bass.ds(b, 1), T * P:(T + 1) * P, :].rearrange("a p n -> p (a n)"),
                                 gate[:, T % HTILES, :]).then_inc(out_st[T % HTILES], 16)

                def slots(b):
                    nb = (b + 1) & (B - 1)
                    for T in range(TILES):
                        m, C, t = b * TILES + T, b * BC + T * HC, T % HTILES
                        pb, pT = (b, 0) if T >= HTILES else (b - 1, HTILES)
                        pm = m - t - HTILES
                        some = not known_first(m, HTILES)
                        load_w1(C + 4, T * HC + 4)
                        load_tl(m + 1, m + 1 if T < TILES - 1 else nb * TILES)
                        if t == 2:
                            load_x(m - 2, b, T - 2)
                            load_x(m - 1, b, T - 1)
                        if T == 0:
                            load_kv(8 * b + GAP, U_VL, b)
                            load_kv(8 * b + GAP + 1, U_VL + 1, b)
                        if T == 1:
                            load_kv(8 * b + GAP + 2, U_VS, b)
                            load_kv(8 * b + GAP + 3, U_VS + 1, b)
                        if T == TILES - 1:
                            load_kv(8 * b + GAP + 4, U_KS, nb)
                            load_kv(8 * b + GAP + 5, U_KS + 1, nb)
                        if t == HTILES - 1:
                            hh = T // HTILES
                            g = KT * (2 * b + hh + 1)
                            nh = 2 * b + 1 if hh == 0 else 2 * nb
                            load_xn(g, 0, nh)
                            load_xn(g + 1, 1, nh)
                        if t == 0 and some:
                            load_x(pm + 2, pb, pT + 2)
                            store(pm, pb, pT)
                        load_w1(C + 5, T * HC + 5)
                        if t == 0 and some:
                            load_x(pm + 3, pb, pT + 3)
                            store(pm + 1, pb, pT + 1)
                        if t == 2 and some:
                            store(pm + 3, pb, pT + 3)
                        load_w1(C + 6, T * HC + 6)
                        if T == TILES - 1:
                            load_kv(8 * b + GAP + 6, U_KL, nb)
                            load_kv(8 * b + GAP + 7, U_KL + 1, nb)
                        if t == 0 and some:
                            store(pm + 2, pb, pT + 2)
                        if t == HTILES - 1:
                            load_xn(g + 2, 2, nh)
                            load_xn(g + 3, 3, nh)
                        load_w1(C + 7, T * HC + 7)

                slots(0)
                with sp.Fori(1, B) as b:
                    slots(b)
                for T in range(HTILES, TILES):
                    m = (B - 1) * TILES + T
                    if T >= HTILES + 2:
                        load_x(m, B - 1, T)
                for T in range(HTILES, TILES):
                    store((B - 1) * TILES + T, B - 1, T)
                for t in range(HTILES):
                    sp.wait_ge(out_st[t], 16 * 2 * B)
                for j in range(2):
                    sp.wait_ge(w1_in[j], 16 * (B * BC // 2 + 2))

            @block.scalar
            def _(act):
                def hi(out_, src, ready):
                    return nc.scalar.activation(out_, src, ACT.Copy).then_inc(ready, 1)

                def split_w1(C, c):
                    act.wait_ge(w1_in[c % 2], 8 * (C - c % 2) + 16)
                    hi(w1_hi[:, c % 2, :, :], w1[:, c % 2, :, :], w1_h)

                def split_kv(g, u):
                    act.wait_ge(kv_in[u % 2], 8 * (g - u % 2) + 16)
                    hi(kv_hi[:, u, :], kv[:, u % 2, :], kv_h)

                def split_xn(g, k):
                    act.wait_ge(xn_in[k % 2], 8 * (g - k % 2) + 16)
                    hi(xnT_hi[:, k, :], xnT[:, k % 2, :], xn_h)

                def split_tl(m, parity):
                    act.wait_ge(tl_in, 16 * m + 16)
                    hi(tl_hi[:, parity, :, :], tl[:, :, :], tl_h)

                def sparse_scores(m, parity):
                    act.wait_ge(ss_done, m + 1)
                    if not known_first(m, 2):
                        act.wait_ge(masked, m - 1)
                    nc.scalar.activation(sc[:, parity, :], scores[:, :], ACT.Copy, scale=SCALE).then_inc(sc_ready, 1)

                def chunk(C, c, h_next):
                    act.wait_ge(f1_done, C + 1)
                    if not known_first(C, 2):
                        act.wait_ge(h_l, C - 1)
                        act.wait_ge(f2_done, C - 1)
                    bias = b1[:, c % CH:c % CH + 1]
                    nc.scalar.activation(h32[:, c % 2, :], hid[:, :], ACT.Relu, bias=bias)
                    nc.scalar.activation(h_hi[:, c % 2, :], hid[:, :], ACT.Relu, bias=bias).then_inc(h_h, 1)
                    hi(w2_hi[:, c % 2, :], w2[:, c % CH, :], w2_h)
                    if c % CH == CH - 1:
                        for k in range(KT):
                            split_xn(KT * h_next + k, k)
                    split_w1(C + 2, c + 2)

                def transposed(i):
                    act.wait_ge(tr_done, i + 1)
                    for j in range(2):
                        if not known_first(i, 1):
                            act.wait_ge(pT_l, 2 * i - 1 + j)
                        c = slice(j * 512, (j + 1) * 512)
                        nc.scalar.activation(pT[:, j, :], scores[:, c], ACT.Copy)
                        nc.scalar.activation(pT_hi[:, c], scores[:, c], ACT.Copy).then_inc(pT_h, 1)

                def head_out(i, head):
                    act.wait_ge(pv_done, i + 1)
                    nc.scalar.activation(at[:, head, :], o[:, 0:P], ACT.Copy)
                    nc.scalar.activation(at_hi[:, head, :], o[:, 0:P], ACT.Copy).then_inc(at_h, 1)

                def gates(h):
                    act.wait_ge(f2_done, CH * (h + 1))
                    for t in range(HTILES):
                        if not known_first(h, 1):
                            act.wait_ge(out_st[t], 16 * h)
                        nc.scalar.activation(gate[:, t, :], acc[:, t, :], ACT.Tanh, scale=0.5).then_inc(tanh_ready, 1)

                def mix(m, t):
                    act.wait_ge(mix_done, m + 1)
                    if not known_first(m, HTILES):
                        act.wait_ge(prod_ready, m - HTILES + 1)
                    nc.scalar.activation(mixed[:, t, :], o[:, :], ACT.Copy, scale=0.5).then_inc(mix_ready, 1)

                split_tl(0, 0)
                split_kv(0, U_KS)
                split_kv(1, U_KS + 1)
                split_w1(0, 0)
                split_w1(1, 1)
                for k in range(KT):
                    split_xn(k, k)
                split_kv(2, U_KL)
                split_kv(3, U_KL + 1)

                def sparse_end(m):
                    act.wait_ge(invs_ready, m + 1)
                    nc.scalar.activation(prob[:, 1, :], prob[:, 1, :], ACT.Copy, scale=inv[:, 1:2]).then_inc(pr_ready, 1)
                    transposed(2 * m + 1)

                def slots(b):
                    for T in range(TILES):
                        m, C, c = b * TILES + T, b * BC + T * HC, T * HC
                        h = 2 * b + T // HTILES
                        some = not known_first(m, 1)
                        sparse_scores(m, T % 2)
                        if T % HTILES == 0 and some:
                            gates(h - 1)
                        chunk(C, c, h + 1)
                        if some:
                            head_out(2 * m - 2, 0)
                        if T == 1:
                            split_kv(8 * b + GAP + 2, U_VS)
                            split_kv(8 * b + GAP + 3, U_VS + 1)
                        if T == TILES - 1:
                            split_kv(8 * b + GAP + 4, U_KS)
                            split_kv(8 * b + GAP + 5, U_KS + 1)
                        if some:
                            sparse_end(m - 1)
                        chunk(C + 1, c + 1, h + 1)
                        act.wait_ge(nms_ready, m + 1)
                        nc.scalar.activation(prob[:, 1, :], sc[:, T % 2, :], ACT.Exp, bias=nms[:, T % 2:T % 2 + 1])\
                            .then_inc(es_ready, 1)
                        if T == 0:
                            split_kv(8 * b + GAP, U_VL)
                            split_kv(8 * b + GAP + 1, U_VL + 1)
                        if some:
                            head_out(2 * m - 1, 1)
                        act.wait_ge(nml_ready, m + 1)
                        nc.scalar.activation(prob[:, 0, :], scores[:, :], ACT.Exp, bias=nml[:, :], scale=SCALE,
                                             accum_out=sums[:, 0:1]).then_inc(el_ready, 1)
                        act.wait_ge(invl_ready, m + 1)
                        nc.scalar.activation(prob[:, 0, :], prob[:, 0, :], ACT.Copy, scale=inv[:, 0:1])\
                            .then_inc(pr_ready, 1)
                        chunk(C + 2, c + 2, h + 1)
                        if T == TILES - 1:
                            split_kv(8 * b + GAP + 6, U_KL)
                            split_kv(8 * b + GAP + 7, U_KL + 1)
                        if some:
                            mix(m - 1, (T - 1) % HTILES)
                        split_tl(m + 1, (T + 1) % 2)
                        transposed(2 * m)
                        chunk(C + 3, c + 3, h + 1)

                slots(0)
                with act.Fori(1, B) as b:
                    slots(b)
                head_out(2 * B * TILES - 2, 0)
                gates(2 * B - 1)
                sparse_end(B * TILES - 1)
                head_out(2 * B * TILES - 1, 1)
                mix(B * TILES - 1, HTILES - 1)

            @block.gpsimd
            def _(pool):
                def lo(out_, value, hi_, ready):
                    return nc.gpsimd.tensor_tensor(out_, value, hi_.bitcast(F32), ALU.subtract).then_inc(ready, 1)

                def split_w1(C, c):
                    pool.wait_ge(w1_h, C + 1)
                    lo(w1_lo[:, c % 2, :, :], w1[:, c % 2, :, :], w1_hi[:, c % 2, :, :], w1_l)

                def split_kv(g, u):
                    pool.wait_ge(kv_h, g + 1)
                    lo(kv_lo[:, u, :], kv[:, u % 2, :], kv_hi[:, u, :], kv_l)

                def split_xn(g, k):
                    pool.wait_ge(xn_h, g + 1)
                    lo(xnT_lo[:, k, :], xnT[:, k % 2, :], xnT_hi[:, k, :], xn_l)

                def split_tl(m, parity):
                    pool.wait_ge(tl_h, m + 1)
                    lo(tl_lo[:, parity, :, :], tl[:, :, :], tl_hi[:, parity, :, :], tl_l)

                def chunk(C, c, h_next):
                    pool.wait_ge(h_h, C + 1)
                    lo(h_lo[:, c % 2, :], h32[:, c % 2, :], h_hi[:, c % 2, :], h_l)
                    pool.wait_ge(w2_h, C + 1)
                    lo(w2_lo[:, c % 2, :], w2[:, c % CH, :], w2_hi[:, c % 2, :], w2_l)
                    if c % CH == CH - 1:
                        for k in range(KT):
                            split_xn(KT * h_next + k, k)
                    split_w1(C + 2, c + 2)

                def transposed(i):
                    for j in range(2):
                        pool.wait_ge(pT_h, 2 * i + j + 1)
                        lo(pT_lo[:, j * 512:(j + 1) * 512], pT[:, j, :], pT_hi[:, j * 512:(j + 1) * 512], pT_l)

                def head_out(i, head):
                    pool.wait_ge(at_h, i + 1)
                    lo(at_lo[:, head, :], at[:, head, :], at_hi[:, head, :], at_l)

                def residual(m, T):
                    t = T % HTILES
                    pool.wait_ge(gate_ready, m + 1)
                    pool.wait_ge(mix_ready, m + 1)
                    nc.gpsimd.tensor_tensor(gate[:, t, :], gate[:, t, :], mixed[:, t, :], ALU.mult)\
                        .then_inc(prod_ready, 1)
                    pool.wait_ge(prod_ready, m + 1)
                    pool.wait_ge(xr_in[T % 2], 8 * (m - T % 2) + 16)
                    nc.gpsimd.tensor_tensor(gate[:, t, :], gate[:, t, :], xin[:, T % 2, :], ALU.add)\
                        .then_inc(fin_ready, 1)

                split_tl(0, 0)
                split_kv(0, U_KS)
                split_kv(1, U_KS + 1)
                split_w1(0, 0)
                split_w1(1, 1)
                for k in range(KT):
                    split_xn(k, k)
                split_kv(2, U_KL)
                split_kv(3, U_KL + 1)

                def slots(b):
                    for T in range(TILES):
                        m, C, c = b * TILES + T, b * BC + T * HC, T * HC
                        h, t = 2 * b + T // HTILES, T % HTILES
                        some = not known_first(m, 1)
                        finish = t == 0 and not known_first(m, HTILES)
                        pm, pT = m - HTILES, (T - HTILES) % TILES
                        chunk(C, c, h + 1)
                        if some:
                            head_out(2 * m - 2, 0)
                        if T == 1:
                            split_kv(8 * b + GAP + 2, U_VS)
                            split_kv(8 * b + GAP + 3, U_VS + 1)
                        if T == TILES - 1:
                            split_kv(8 * b + GAP + 4, U_KS)
                            split_kv(8 * b + GAP + 5, U_KS + 1)
                        if finish:
                            residual(pm, pT)
                        if some:
                            transposed(2 * m - 1)
                        chunk(C + 1, c + 1, h + 1)
                        if T == 0:
                            split_kv(8 * b + GAP, U_VL)
                            split_kv(8 * b + GAP + 1, U_VL + 1)
                        if finish:
                            residual(pm + 1, pT + 1)
                        if some:
                            head_out(2 * m - 1, 1)
                        chunk(C + 2, c + 2, h + 1)
                        if T == TILES - 1:
                            split_kv(8 * b + GAP + 6, U_KL)
                            split_kv(8 * b + GAP + 7, U_KL + 1)
                        if finish:
                            residual(pm + 2, pT + 2)
                        if t == 1 and not known_first(m, HTILES):
                            residual(m - 2, (T - 2) % TILES)
                        split_tl(m + 1, (T + 1) % 2)
                        transposed(2 * m)
                        chunk(C + 3, c + 3, h + 1)

                slots(0)
                with pool.Fori(1, B) as b:
                    slots(b)
                head_out(2 * B * TILES - 2, 0)
                transposed(2 * B * TILES - 1)
                head_out(2 * B * TILES - 1, 1)
                for T in range(HTILES, TILES):
                    residual((B - 1) * TILES + T, T)

            @block.vector
            def _(dve):
                def apply_threshold(m, parity):
                    dve.wait_ge(es_ready, m + 1)
                    nc.vector.scalar_tensor_tensor(out=prob[:, 1, :], in0=sc[:, parity, :],
                                                   scalar=m8[:, (TOPK - 1) % 8:(TOPK - 1) % 8 + 1],
                                                   in1=prob[:, 1, :], op0=ALU.is_ge, op1=ALU.mult,
                                                   accum_out=sums[:, 1:2]).then_inc(masked, 1)
                    dve.wait_ge(masked, m + 1)
                    nc.vector.reciprocal(inv[:, 1:2], sums[:, 1:2]).then_inc(invs_ready, 1)

                def gates(h):
                    for t in range(HTILES):
                        dve.wait_ge(tanh_ready, HTILES * h + t + 1)
                        nc.vector.scalar_tensor_tensor(out=gate[:, t, :], in0=gate[:, t, :], scalar=1.0,
                                                       in1=acc[:, t, :], op0=ALU.add, op1=ALU.mult)\
                            .then_inc(gate_ready, 1)

                def full_max(m):
                    dve.wait_ge(sl_done, m + 1)
                    nc.vector.tensor_reduce(mxl[:, :], scores[:, :], AX_X, ALU.max).then_inc(nml_step, 1)
                    dve.wait_ge(nml_step, m + 1)
                    nc.vector.tensor_scalar(nml[:, :], mxl[:, :], -SCALE, None, ALU.mult).then_inc(nml_ready, 1)

                def full_inverse(m):
                    dve.wait_ge(el_ready, m + 1)
                    nc.vector.reciprocal(inv[:, 0:1], sums[:, 0:1]).then_inc(invl_ready, 1)

                def search(m, T, b):
                    done = 1 + STEPS * T
                    dve.wait_ge(step, done)
                    wait_alone(dve, sc_ready, m + 1, dve_passed)
                    for r in range(ROUNDS):
                        src = sc[:, T % 2, :] if r == 0 else work[:, :]
                        nc.vector.max(m8[:, :], src).then_inc(step, 1)
                        dve.wait_ge(step, done + 2 * r + 1)
                        if r == 0:
                            nc.vector.tensor_scalar(nms[:, T % 2:T % 2 + 1], m8[:, 0:1], -1.0, None, ALU.mult)\
                                .then_inc(nms_ready, 1)
                        if r < ROUNDS - 1:
                            nc.vector.match_replace(work[:, :], m8[:, :], src, LOWEST).then_inc(step, 1)
                            dve.wait_ge(step, done + 2 * r + 2)
                        if r == 1 and T % HTILES == 0 and not known_first(m, 1):
                            gates(2 * b + T // HTILES - 1)
                        if r == 6:
                            full_max(m)
                        if r == 7:
                            full_inverse(m)

                def slots(b):
                    for T in range(TILES):
                        m = b * TILES + T
                        if not known_first(m, 1):
                            apply_threshold(m - 1, (T - 1) % 2)
                        if T == 0:
                            if not known_first(m, 1):
                                nc.vector.sem_clear(step)
                            nc.vector.memset(m8[:, :], LOWEST).then_inc(step, 1)
                        search(m, T, b)

                slots(0)
                with dve.Fori(1, B) as b:
                    slots(b)
                apply_threshold(B * TILES - 1, 1)
                gates(2 * B - 1)

            @block.tensor
            def _(pe):
                def f1(C, c, h):
                    pe.wait_ge(w1_l, C + 1)
                    if not known_first(C, 1):
                        pe.wait_ge(h_h, C)
                    for k in range(KT):
                        if c % CH == 0:
                            pe.wait_ge(xn_l, KT * h + k + 1)
                        last = product(nc, hid[:, :], w1_hi[:, c % 2, k, :], w1_lo[:, c % 2, k, :],
                                       xnT_hi[:, k, :], xnT_lo[:, k, :], k == 0, k == KT - 1)
                    last.then_inc(f1_done, 1)

                def f2(C, c, h):
                    pe.wait_ge(h_l, C + 1)
                    pe.wait_ge(w2_l, C + 1)
                    start = c % CH == 0
                    if start and not known_first(C, 1):
                        pe.wait_ge(gate_ready, HTILES * h)
                    for t in range(HTILES):
                        last = product(nc, acc[:, t, :], h_hi[:, c % 2, t * P:(t + 1) * P],
                                       h_lo[:, c % 2, t * P:(t + 1) * P], w2_hi[:, c % 2, :], w2_lo[:, c % 2, :],
                                       start, False)
                        if c % CH == CH - 1:
                            nc.tensor.matmul(acc[:, t, :], pick[:, 1, :], rows_hi[:, :], start=False, stop=False)
                            last = nc.tensor.matmul(acc[:, t, :], pick[:, 1, :], rows_lo[:, :], start=False, stop=True)
                    last.then_inc(f2_done, 1)

                def head_scores(parity, slot, unit, done):
                    for j in range(2):
                        last = product(nc, scores[:, j * 512:(j + 1) * 512], tl_hi[:, parity, slot, :],
                                       tl_lo[:, parity, slot, :], kv_hi[:, unit + j, :], kv_lo[:, unit + j, :],
                                       True, True)
                    last.then_inc(done, 1)

                def transposes(i, head):
                    pe.wait_ge(pr_ready, i + 1)
                    for j in range(TILES):
                        last = nc.tensor.transpose(scores[:, j * P:(j + 1) * P], prob[:, head, j * P:(j + 1) * P],
                                                   ident[:, :])
                    last.then_inc(tr_done, 1)

                def head_out(i, unit):
                    pe.wait_ge(pT_l, 2 * i + 2)
                    for j in range(TILES):
                        u, c = unit + j // HTILES, slice((j % HTILES) * P, (j % HTILES + 1) * P)
                        last = product(nc, o[:, 0:P], kv_hi[:, u, c], kv_lo[:, u, c], pT_hi[:, j * P:(j + 1) * P],
                                       pT_lo[:, j * P:(j + 1) * P], j == 0, j == TILES - 1)
                    last.then_inc(pv_done, 1)

                def sparse_head_out(m, b_kv):
                    pe.wait_ge(at_h, 2 * m + 1)
                    pe.wait_ge(kv_l, b_kv)
                    head_out(2 * m + 1, U_VS)

                def mix(m, parity):
                    pe.wait_ge(at_l, 2 * m + 2)
                    for j in range(2):
                        product(nc, o[:, :], at_hi[:, j, :], at_lo[:, j, :], ww_hi[:, j, :], ww_lo[:, j, :],
                                j == 0, False)
                    for j in (T_MEM, T_PRED):
                        product(nc, o[:, :], tl_hi[:, parity, j, :], tl_lo[:, parity, j, :], ww_hi[:, j, :],
                                ww_lo[:, j, :], False, False)
                    nc.tensor.matmul(o[:, :], pick[:, 0, :], rows_hi[:, :], start=False, stop=False)
                    nc.tensor.matmul(o[:, :], pick[:, 0, :], rows_lo[:, :], start=False, stop=True)\
                        .then_inc(mix_done, 1)

                def sparse_scores(m, parity, kv_count):
                    pe.wait_ge(tl_l, m + 1)
                    if kv_count is not None:
                        pe.wait_ge(kv_l, kv_count)
                    head_scores(parity, T_QS, U_KS, ss_done)

                def slots(b):
                    for T in range(TILES):
                        m, C, c = b * TILES + T, b * BC + T * HC, T * HC
                        h, t = 2 * b + T // HTILES, T % HTILES
                        some = not known_first(m, 1)
                        if some:
                            pe.wait_ge(pT_h, 4 * m - 2)
                        sparse_scores(m, T % 2, 8 * b + 2 if T == 0 else None)
                        f1(C, c, h)
                        if some:
                            if not known_first(m, 2):
                                pe.wait_ge(mix_ready, m - 1)
                            head_out(2 * m - 2, U_VL)
                        if t > 0:
                            f2(C - 1, c - 1, h)
                        pe.wait_ge(sc_ready, m + 1)
                        if some:
                            transposes(2 * m - 1, 1)
                        f1(C + 1, c + 1, h)
                        if some:
                            pe.wait_ge(pT_h, 4 * m)
                        if T == 0:
                            pe.wait_ge(kv_l, 8 * b + GAP)
                        head_scores(T % 2, T_QL, U_KL, sl_done)
                        f2(C, c, h)
                        if some:
                            sparse_head_out(m - 1, 8 * b + GAP + (4 if T > 0 else 0))
                        f1(C + 2, c + 2, h)
                        f2(C + 1, c + 1, h)
                        if some:
                            mix(m - 1, (T + 1) % 2)
                        transposes(2 * m, 0)
                        f1(C + 3, c + 3, h)
                        f2(C + 2, c + 2, h)
                        if t == HTILES - 1:
                            f2(C + 3, c + 3, h)

                slots(0)
                with pe.Fori(1, B) as b:
                    slots(b)
                m = B * TILES - 1
                pe.wait_ge(mix_ready, m)
                head_out(2 * m, U_VL)
                pe.wait_ge(pT_h, 4 * m + 2)
                transposes(2 * m + 1, 1)
                sparse_head_out(m, 8 * B + GAP)
                mix(m, m % 2)


def program(nc, ins, out):
    names = {n.removeprefix("L0_attn_").removeprefix("L0_ffn_"): a for n, a in ins.items()}
    build(nc, names["x"], names, out)


_OUT = ((B, S, D), "float32")
_ORDER = ["L0_attn_x", "L0_attn_local_qkv_w", "L0_attn_sparse_qkv_w", "L0_attn_memory_bank",
          "L0_attn_memory_proj_w", "L0_attn_mem_out_w", "L0_attn_mem_out_b", "L0_attn_pred_in_w",
          "L0_attn_pred_in_b", "L0_attn_pred1_w", "L0_attn_pred1_b", "L0_attn_pred2_w", "L0_attn_pred2_b",
          "L0_attn_warboss_w", "L0_attn_warboss_b", "L0_ffn_w1", "L0_ffn_b1", "L0_ffn_w2", "L0_ffn_b2"]


def kernel(**inputs):
    import numpy as _np
    import concourse.bacc as _bacc
    from concourse import mybir as _mybir
    from concourse.bass_utils import run_bass_kernel_spmd as _run

    nc = _bacc.Bacc("TRN2", target_bir_lowering=False, num_devices=1)
    arrays, args = {}, {}
    for name in _ORDER:
        a = _np.ascontiguousarray(inputs[name])
        arrays[f"in_{name}"] = a
        args[name] = nc.dram_tensor(f"in_{name}", a.shape, _mybir.dt.from_np(a.dtype), kind="ExternalInput").ap()
    shape, dtype = _OUT
    out = nc.dram_tensor("out_0", shape, _mybir.dt.from_np(_np.dtype(dtype)), kind="ExternalOutput").ap()
    program(nc, args, out)
    r = _run(nc, [arrays], core_ids=[0])
    return r.results[0]["out_0"]
```

```python
from contextlib import ExitStack

import concourse.bass as bass
from concourse import mybir

F32 = mybir.dt.float32
F32R = mybir.dt.float32r
I32 = mybir.dt.int32
ALU = mybir.AluOpType
ACT = mybir.ActivationFunctionType
AX_X = mybir.AxisListType.X

P = 128
B, S, D = 8, 1024, 512
HD, MEM = 128, 64
WIDTH = 2048
KT = D // P
HALF = 512
TILES = S // P
HTILES = HALF // P
CH = WIDTH // P
TOPK = max(1, int(S * 0.1))
ROUNDS = (TOPK + 7) // 8
ROUNDS_S = (TOPK // 2 + 7) // 8
SCALE = HD ** -0.5
EPS = 1e-5
LOWEST, HIGHEST = -3.0e38, 3.0e38
RSQRT_SEED = float(0x5F3759DF)
NEWTON = 3
LO_ROW = 32

MP, PI, QL, QS, KL, KS, VL, VS = range(8)
JOBS = ["mp", "pi", "ql", "ms", "p1a", "p1b", "qs", "wt", "kl", "ret", "p2", "ks",
        "tr0", "tr1", "tr2", "tr3", "v01", "v23", "mo"]
NJ = len(JOBS)
BANKS = 8
U_KS, U_KL, U_VL, U_VS = 0, 2, 4, 6
T_QL, T_QS, T_MEM, T_PRED = range(4)


def wait_alone(eng, sem, value, passed):
    eng.wait_ge(sem, value)
    eng.sem_inc(passed, 1)


def product(nc, out, w_hi, w_lo, x_hi, x_lo, first, last):
    nc.tensor.matmul(out, w_hi, x_hi, start=first, stop=False)
    nc.tensor.matmul(out, w_hi, x_lo, start=False, stop=False)
    return nc.tensor.matmul(out, w_lo, x_hi, start=False, stop=last)


def build(nc, x, w, out):
    xnT_d = nc.dram_tensor("xnT_scratch", [2 * B, P, KT, HALF], F32)
    kv_d = nc.dram_tensor("kv_scratch", [B, P, 8, HALF], F32)
    tile_d = nc.dram_tensor("tile_scratch", [B * TILES, P, 4, P], F32)
    with ExitStack() as outer:
        def sb(name, shape, dt):
            return outer.enter_context(nc.sbuf_tensor(name, shape, dt))

        ident = sb("ident", [P, P], F32)
        ww_hi = sb("ww_hi", [P, KT, D], F32R)
        ww_lo = sb("ww_lo", [P, KT, D], F32R)
        rows = sb("rows", [P, D], F32R)
        pick = sb("pick", [P, 2, P], F32R)
        w2 = sb("w2", [P, CH, D], F32)
        b1 = sb("b1", [P, CH], F32)
        stage1(nc, x, w, xnT_d, kv_d, tile_d, ident, ww_hi, ww_lo, rows, pick, w2, b1)
        stage2(nc, x, w, xnT_d, kv_d, tile_d, ident, ww_hi, ww_lo, rows, pick, w2, b1, out)


def stage1(nc, x, w, xnT_d, kv_d, tile_d, ident, ww_hi, ww_lo, rows, pick, w2, b1):
    XP, PIN, WT, RET = range(4)
    LO = ["xp", "pin", "gelu", "wt", "ret"]
    KV_SLOT = {"ks": 0, "kl": 1}
    PER = 2 * NJ
    SM_LOADS = 9
    CONSTS = 7
    WK_LOADS = 4

    with ExitStack() as ctx:
        def sb(name, shape, dt):
            return ctx.enter_context(nc.sbuf_tensor(name, shape, dt))

        def sem(name):
            return ctx.enter_context(nc.semaphore(name))

        wp_hi = sb("wp_hi", [P, KT, 8 * P], F32R)
        wp_lo = sb("wp_lo", [P, KT, 8 * P], F32R)
        staged = w2[:, :, :].rearrange("p c n -> p (c n)")
        wp = staged[:, 0:KT * 8 * P].rearrange("p (k n) -> p k n", k=KT)
        ww = staged[:, KT * 8 * P:KT * 8 * P + KT * D].rearrange("p (k n) -> p k n", k=KT)
        sm = sb("sm", [P, 7, P], F32)
        sm_hi = sb("sm_hi", [P, 7, P], F32R)
        sm_lo = sb("sm_lo", [P, 7, P], F32R)
        bkT = sb("bkT", [P, MEM], F32)
        bkT_hi = sb("bkT_hi", [P, MEM], F32R)
        bkT_lo = sb("bkT_lo", [P, MEM], F32R)
        pick32 = sb("pick32", [P, 2, P], F32)
        rows32 = sb("rows32", [P, D], F32)
        b_pi = sb("b_pi", [P, 1], F32)
        b_p1 = sb("b_p1", [P, 2], F32)
        b_p2 = sb("b_p2", [P, 1], F32)
        b_mo = sb("b_mo", [P, 1], F32)
        xin = sb("xin1", [P, HTILES, D], F32)
        stats = sb("stats", [P, HTILES, 6], F32)
        mv = sb("mv", [P, HTILES, 2], F32)
        var = sb("var", [P, HTILES], F32)
        rstd = sb("rstd", [P, HTILES], F32)
        nt = sb("nt", [P, HTILES], F32)
        xn = sb("xn", [P, HTILES, D], F32)
        xnT = sb("xnT1", [P, KT, HALF], F32)
        xnT_hi = sb("xnT1_hi", [P, 2, KT, HALF], F32R)
        xnT_lo = sb("xnT1_lo", [P, 2, KT, HALF], F32R)
        act32 = sb("act32", [P, 2, HALF], F32)
        act_hi = sb("act_hi", [P, 4, HALF], F32R)
        act_lo = sb("act_lo", [P, 4, HALF], F32R)
        gelu = sb("gelu", [P, 2, HALF], F32)
        gelu_hi = sb("gelu_hi", [P, 2, HALF], F32R)
        gelu_lo = sb("gelu_lo", [P, 2, HALF], F32R)
        nmx = sb("nmx", [P, HTILES], F32)
        esum = sb("esum", [P, HTILES], F32)
        einv = sb("einv", [P, HTILES], F32)
        we = sb("we", [P, HTILES, MEM], F32)
        tiles_out = sb("tiles_out", [P, HTILES, 4, P], F32)
        kv_out = sb("kv_out", [P, 4, HALF], F32)
        ps = ctx.enter_context(nc.psum_tensor("ps1", [P, BANKS, 512], F32))

        w_in = [sem(f"w_in{k}") for k in range(KT)]
        ww_in = sem("ww_in")
        sm_in = sem("sm_in")
        rows_in = sem("rows_in")
        w2_in = sem("w2_in")
        consts = sem("consts")
        w_h = sem("w_h")
        w_split = sem("w_split")
        rows_h = sem("rows_h")
        sm_split = sem("sm_split")
        bkT_ps = sem("bkT_ps")
        bkT_out = sem("bkT_out")
        bkT_split = sem("bkT_split")
        x_in = sem("x_in")
        ln_step = sem("ln_step")
        xn_ready = sem("xn_ready")
        job_done = sem("job_done")
        bank_read = sem("bank_read")
        lo_ready = sem("lo_ready")
        ghi_ready = sem("ghi_ready")
        xlo_ready = sem("xlo_ready")
        max_ready = sem("max_ready")
        inv_ready = sem("inv_ready")
        wn_ready = sem("wn_ready")
        tiles_st = sem("tiles_st")
        kv_st = sem("kv_st")
        xnT_st = sem("xnT_st")
        sp_passed, pe_passed = sem("sp1_passed"), sem("pe_passed")

        def done(n, name):
            return KT + n * NJ + JOBS.index(name) + 1

        def bank(hh, name):
            return (KT + hh * NJ + JOBS.index(name)) % BANKS

        def bank_free(b, hh, name):
            p = hh * NJ + JOBS.index(name)
            own = [q for q in range(-KT, p) if (q - p) % BANKS == 0]
            if isinstance(b, int):
                return KT + own[-1] + 1 if own else None
            near = max(q for q in range(p - BANKS - PER, p) if
                       (q >= 0 and (q - p) % BANKS == 0) or (q < 0 and (q + PER - p) % BANKS == 0))
            return KT + b * PER + near + 1

        def lo(n, name):
            return n * len(LO) + LO.index(name) + 1

        def first(n):
            return isinstance(n, int) and n == 0

        with nc.Block() as block:
            @block.sync
            def _(sp):
                lq, sq = w["local_qkv_w"], w["sparse_qkv_w"]
                sp.dma_start(xin[:, :, :], x[0, 0:HALF, :].rearrange("(t p) d -> p t d", p=P)).then_inc(x_in, 16)
                for k in range(KT):
                    r = slice(k * P, (k + 1) * P)
                    sp.dma_start(wp[:, k, 0:P], w["memory_proj_w"][r, :]).then_inc(w_in[k], 16)
                    sp.dma_start(wp[:, k, P:2 * P], w["pred_in_w"][r, :]).then_inc(w_in[k], 16)
                    pairs = wp[:, k, 2 * P:8 * P].rearrange("p (i h n) -> p i h n", h=2, n=P)
                    for head, weights in enumerate((lq, sq)):
                        sp.dma_start(pairs[:, :, head, :], weights[r, :].rearrange("p (i n) -> p i n", n=P))\
                            .then_inc(w_in[k], 16)
                sp.dma_start(ww[:, :, :], w["warboss_w"].rearrange("(k p) n -> p k n", p=P)).then_inc(ww_in, 16)
                sp.wait_ge(xn_ready, 1)
                sp.dma_start(xin[:, :, :], x[0, HALF:S, :].rearrange("(t p) d -> p t d", p=P)).then_inc(x_in, 16)
                sp.wait_ge(w_split, 2 * KT)
                sp.dma_start(w2[:, :, :], w["w2"].rearrange("(c p) n -> p c n", p=P)).then_inc(w2_in, 16)

                def steps(b):
                    for hh in range(2):
                        n = 2 * b + hh
                        nb = (b + 1) & (B - 1)
                        wait_alone(sp, xn_ready, n + 2, sp_passed)
                        sp.dma_start(xin[:, :, :],
                                     x[bass.ds(nb, 1), hh * HALF:(hh + 1) * HALF, :]
                                     .rearrange("a (t p) d -> p (a t) d", p=P)).then_inc(x_in, 16)
                        sp.wait_ge(bank_read, KT if first(n) else done(n - 1, "tr3"))
                        sp.dma_start(xnT_d[bass.ds(n, 1), :, :, :].rearrange("a p k n -> p (a k) n"),
                                     xnT[:, :, :]).then_inc(xnT_st, 16)
                        wait_alone(sp, bank_read, done(n, "v23"), sp_passed)
                        sp.dma_start(kv_d[bass.ds(b, 1), :, :, :]
                                     .rearrange("a p (u h) n -> p (a u) h n", h=2)[:, :, hh, :],
                                     kv_out[:, :, :]).then_inc(kv_st, 16)
                        sp.wait_ge(bank_read, done(n, "mo"))
                        sp.dma_start(tile_d[bass.ds(n * HTILES, HTILES), :, :, :].rearrange("t p s n -> p t (s n)"),
                                     tiles_out[:, :, :, :].rearrange("p t s n -> p t (s n)")).then_inc(tiles_st, 16)

                steps(0)
                with sp.Fori(1, B) as b:
                    steps(b)
                sp.wait_ge(xnT_st, 16 * 2 * B)
                sp.wait_ge(kv_st, 16 * 2 * B)
                sp.wait_ge(tiles_st, 16 * 2 * B)
                sp.wait_ge(w2_in, 16)

            @block.gpsimd
            def _(pool):
                pool.memset(rows32[:, :], 0.0).then_inc(consts, 1)
                pool.wait_ge(consts, 1)
                pool.memset(sm[MEM:P, 6, :], 0.0).then_inc(consts, 1)
                pool.wait_ge(consts, 2)
                pool.memset(ident[:, :], 0.0).then_inc(consts, 1)
                pool.wait_ge(consts, 3)
                pool.memset(pick32[:, :, :], 0.0).then_inc(consts, 1)
                pool.wait_ge(consts, 4)
                pool.affine_select(out=ident[:, :], in_=ident[:, :], compare_op=ALU.not_equal, fill=1.0,
                                   base=0, pattern=[[-1, P]], channel_multiplier=1).then_inc(consts, 1)
                for i, row in enumerate((0, LO_ROW)):
                    pool.wait_ge(consts, 5 + i)
                    pool.affine_select(out=pick32[:, :, :], in_=pick32[:, :, :], compare_op=ALU.not_equal, fill=1.0,
                                       base=-row, pattern=[[-1, 2], [0, P]], channel_multiplier=1).then_inc(consts, 1)
                for k in range(2 * KT):
                    pool.wait_ge(w_h, k + 1)
                    lo_, src, hi = ((wp_lo[:, k, :], wp[:, k, :], wp_hi[:, k, :]) if k < KT else
                                    (ww_lo[:, k - KT, :], ww[:, k - KT, :], ww_hi[:, k - KT, :]))
                    pool.tensor_tensor(lo_, src, hi.bitcast(F32), ALU.subtract).then_inc(w_split, 1)

            @block.scalar
            def _(act):
                def column(name):
                    return w[name].rearrange("(p a) -> p a", a=1)

                act.dma_start(sm[:, 0:2, :], w["mem_out_w"].rearrange("(k p) n -> p k n", p=P)).then_inc(sm_in, 16)
                act.dma_start(sm[:, 2:4, :], w["pred1_w"].rearrange("p (k n) -> p k n", k=2)).then_inc(sm_in, 16)
                act.dma_start(sm[:, 4:6, :], w["pred2_w"].rearrange("(k p) n -> p k n", p=P)).then_inc(sm_in, 16)
                act.dma_start(sm[0:MEM, 6, :], w["memory_bank"]).then_inc(sm_in, 16)
                act.dma_start(b_pi[:, :], column("pred_in_b")).then_inc(sm_in, 16)
                act.dma_start(b_p2[:, :], column("pred2_b")).then_inc(sm_in, 16)
                act.dma_start(b_mo[:, :], column("mem_out_b")).then_inc(sm_in, 16)
                with nc.allow_non_contiguous_dma(reason="biases by column"):
                    act.dma_start(b_p1[:, :], w["pred1_b"].rearrange("(k p) -> p k", p=P)).then_inc(sm_in, 16)
                    act.dma_start(b1[:, :], w["b1"].rearrange("(k p) -> p k", p=P)).then_inc(sm_in, 16)
                act.wait_ge(consts, 1)
                for row, bias in ((0, "warboss_b"), (1, "b2"), (LO_ROW, "warboss_b"), (LO_ROW + 1, "b2")):
                    act.dma_start(rows32[row:row + 1, :], w[bias].rearrange("(a n) -> a n", a=1)).then_inc(rows_in, 16)
                for k in range(KT):
                    act.wait_ge(w_in[k], 16 * WK_LOADS)
                    nc.scalar.activation(wp_hi[:, k, :], wp[:, k, :], ACT.Copy).then_inc(w_h, 1)
                act.wait_ge(bkT_ps, 1)
                nc.scalar.activation(bkT[:, :], ps[:, BANKS - 1, 0:MEM], ACT.Copy)
                nc.scalar.activation(bkT_hi[:, :], ps[:, BANKS - 1, 0:MEM], ACT.Copy).then_inc(bkT_out, 1)
                act.wait_ge(sm_in, 16 * SM_LOADS)

                for k in range(KT):
                    act.wait_ge(job_done, k + 1)
                    nc.scalar.activation(xnT[:, k, :], ps[:, k, :], ACT.Copy)
                    nc.scalar.activation(xnT_hi[:, 0, k, :], ps[:, k, :], ACT.Copy).then_inc(bank_read, 1)
                act.wait_ge(ww_in, 16)
                for k in range(KT):
                    nc.scalar.activation(ww_hi[:, k, :], ww[:, k, :], ACT.Copy).then_inc(w_h, 1)

                def steps(b):
                    for hh in range(2):
                        n = 2 * b + hh
                        for name in JOBS:
                            src = ps[:, bank(hh, name), :]
                            act.wait_ge(job_done, done(n, name))
                            if name == "mp":
                                nc.scalar.activation(act32[:, XP, :], src, ACT.Copy)
                                last = nc.scalar.activation(act_hi[:, XP, :], src, ACT.Copy)
                            elif name == "pi":
                                nc.scalar.activation(act32[:, PIN, :], src, ACT.Identity, bias=b_pi[:, :])
                                last = nc.scalar.activation(act_hi[:, PIN, :], src, ACT.Identity, bias=b_pi[:, :])
                            elif name == "ret":
                                nc.scalar.activation(act32[:, RET % 2, :], src, ACT.Copy)
                                last = nc.scalar.activation(act_hi[:, RET, :], src, ACT.Copy)
                            elif name == "wt":
                                src = ps[0:MEM, bank(hh, name), :]
                                nc.scalar.activation(act32[0:MEM, WT % 2, :], src, ACT.Copy)
                                last = nc.scalar.activation(act_hi[0:MEM, WT, :], src, ACT.Copy)
                            elif name == "ms":
                                act.wait_ge(max_ready, n + 1)
                                for t in range(HTILES):
                                    last = nc.scalar.activation(we[:, t, :], src[:, t * MEM:(t + 1) * MEM], ACT.Exp,
                                                                bias=nmx[:, t:t + 1], accum_out=esum[:, t:t + 1])
                            elif name in ("p1a", "p1b"):
                                c = int(name == "p1b")
                                last = nc.scalar.activation(gelu[:, c, :], src, ACT.Gelu, bias=b_p1[:, c:c + 1])
                            elif name in ("ql", "qs", "p2", "mo"):
                                if name == "ql" and not first(n):
                                    act.wait_ge(tiles_st, 16 * n)
                                slot = {"ql": T_QL, "qs": T_QS, "p2": T_PRED, "mo": T_MEM}[name]
                                dst = tiles_out[:, :, slot, :]
                                src = src.rearrange("p (t n) -> p t n", n=P)
                                if name in ("p2", "mo"):
                                    bias = b_p2 if name == "p2" else b_mo
                                    last = nc.scalar.activation(dst, src, ACT.Identity, bias=bias[:, :])
                                else:
                                    last = nc.scalar.activation(dst, src, ACT.Copy)
                            elif name in ("kl", "ks"):
                                if name == "kl" and not first(n):
                                    act.wait_ge(kv_st, 16 * n)
                                last = nc.scalar.activation(kv_out[:, KV_SLOT[name], :], src, ACT.Copy)
                            elif name in ("v01", "v23"):
                                c = 2 * P * int(name == "v23")
                                last = nc.scalar.activation(
                                    kv_out[:, 2:4, c:c + 2 * P].rearrange("p h (t n) -> p t h n", n=P),
                                    src.rearrange("p (t h n) -> p t h n", t=2, h=2), ACT.Copy)
                            else:
                                k = int(name[2])
                                if k == 0:
                                    act.wait_ge(xnT_st, 16 * (n + 1))
                                    act.wait_ge(xlo_ready, KT * (n + 1))
                                nc.scalar.activation(xnT[:, k, :], src, ACT.Copy)
                                last = nc.scalar.activation(xnT_hi[:, 1 - hh, k, :], src, ACT.Copy)
                            last.then_inc(bank_read, 1)

                steps(0)
                with act.Fori(1, B) as b:
                    steps(b)

            @block.vector
            def _(dve):
                def subtract(out, value, hi):
                    return nc.vector.tensor_tensor(out, value, hi.bitcast(F32), ALU.subtract)

                def layer_norm(n):
                    if not first(n):
                        nc.vector.sem_clear(ln_step)
                    dve.wait_ge(x_in, 16 * (n + 1))
                    step = [0]

                    def link(ins):
                        ins.then_inc(ln_step, 1)
                        step[0] = step[0] + 1
                        dve.wait_ge(ln_step, step[0])

                    for t in range(HTILES):
                        last = nc.vector.bn_stats(stats[:, t, :], xin[:, t, :])
                    link(last)
                    for t in range(HTILES):
                        last = nc.vector.bn_aggr(mv[:, t, :], stats[:, t, :])
                    link(last)
                    link(nc.vector.tensor_scalar(var[:, :], mv[:, :, 1], EPS, None, ALU.add))
                    link(nc.vector.tensor_scalar(rstd[:, :].bitcast(I32), var[:, :].bitcast(I32),
                                                 -0.5, RSQRT_SEED, ALU.mult, ALU.add))
                    link(nc.vector.tensor_scalar(var[:, :], var[:, :], -0.5, None, ALU.mult))
                    for _ in range(NEWTON):
                        link(nc.vector.tensor_tensor(nt[:, :], rstd[:, :], rstd[:, :], ALU.mult))
                        link(nc.vector.tensor_tensor(nt[:, :], nt[:, :], var[:, :], ALU.mult))
                        link(nc.vector.scalar_tensor_tensor(out=rstd[:, :], in0=nt[:, :], scalar=1.5, in1=rstd[:, :],
                                                            op0=ALU.add, op1=ALU.mult))
                    for t in range(HTILES):
                        last = nc.vector.tensor_scalar(xn[:, t, :], xin[:, t, :], mv[:, t, 0:1],
                                                       rstd[:, t:t + 1], ALU.subtract, ALU.mult)
                    last.then_inc(xn_ready, 1)

                dve.wait_ge(sm_in, 16 * SM_LOADS)
                dve.wait_ge(consts, CONSTS)
                nc.vector.tensor_copy(sm_hi[:, :, :], sm[:, :, :]).then_inc(sm_split, 1)
                dve.wait_ge(sm_split, 1)
                subtract(sm_lo[:, :, :], sm[:, :, :], sm_hi[:, :, :]).then_inc(sm_split, 1)
                layer_norm(0)
                for k in range(KT):
                    dve.wait_ge(bank_read, k + 1)
                    subtract(xnT_lo[:, 0, k, :], xnT[:, k, :], xnT_hi[:, 0, k, :]).then_inc(xlo_ready, 1)
                dve.wait_ge(bkT_out, 1)
                subtract(bkT_lo[:, :], bkT[:, :], bkT_hi[:, :]).then_inc(bkT_split, 1)
                dve.wait_ge(rows_in, 16 * 4)
                dve.wait_ge(consts, CONSTS)
                nc.vector.tensor_copy(pick[:, :, :], pick32[:, :, :])
                nc.vector.tensor_copy(rows[:, :], rows32[:, :]).then_inc(rows_h, 1)
                dve.wait_ge(rows_h, 1)
                lo_rows = slice(LO_ROW, 2 * LO_ROW)
                subtract(rows[lo_rows, :], rows32[lo_rows, :], rows[lo_rows, :])
                layer_norm(1)

                def steps(b):
                    for hh in range(2):
                        n = 2 * b + hh
                        for name, slot in (("mp", XP), ("pi", PIN)):
                            dve.wait_ge(bank_read, done(n, name))
                            subtract(act_lo[:, slot, :], act32[:, slot, :], act_hi[:, slot, :]).then_inc(lo_ready, 1)
                        dve.wait_ge(job_done, done(n, "ms"))
                        nc.vector.tensor_reduce(nmx[:, :], ps[:, bank(hh, "ms"), 0:HTILES * MEM]
                                                .rearrange("p (t m) -> p t m", m=MEM), AX_X, ALU.max,
                                                negate=True).then_inc(max_ready, 1)
                        dve.wait_ge(bank_read, done(n, "ms"))
                        nc.vector.reciprocal(einv[:, :], esum[:, :]).then_inc(inv_ready, 1)
                        dve.wait_ge(inv_ready, n + 1)
                        for t in range(HTILES):
                            last = nc.vector.tensor_scalar(we[:, t, :], we[:, t, :], einv[:, t:t + 1], None, ALU.mult)
                        last.then_inc(wn_ready, 1)
                        dve.wait_ge(bank_read, done(n, "p1b"))
                        nc.vector.tensor_copy(gelu_hi[:, :, :], gelu[:, :, :]).then_inc(ghi_ready, 1)
                        dve.wait_ge(ghi_ready, n + 1)
                        subtract(gelu_lo[:, :, :], gelu[:, :, :], gelu_hi[:, :, :]).then_inc(lo_ready, 1)
                        dve.wait_ge(bank_read, done(n, "wt"))
                        subtract(act_lo[0:MEM, WT, :], act32[0:MEM, WT % 2, :], act_hi[0:MEM, WT, :]).then_inc(lo_ready, 1)
                        dve.wait_ge(bank_read, done(n, "ret"))
                        subtract(act_lo[:, RET, :], act32[:, RET % 2, :], act_hi[:, RET, :]).then_inc(lo_ready, 1)
                        for k in range(KT):
                            dve.wait_ge(bank_read, done(n, f"tr{k}"))
                            subtract(xnT_lo[:, 1 - hh, k, :], xnT[:, k, :], xnT_hi[:, 1 - hh, k, :])\
                                .then_inc(xlo_ready, 1)
                        layer_norm(n + 2)

                steps(0)
                with dve.Fori(1, B) as b:
                    steps(b)

            @block.tensor
            def _(pe):
                pe.wait_ge(sm_in, 16 * SM_LOADS)
                pe.wait_ge(consts, CONSTS)
                nc.tensor.transpose(ps[:, BANKS - 1, 0:MEM], sm[0:MEM, 6, :], ident[0:MEM, 0:MEM]).then_inc(bkT_ps, 1)

                def transposes(k, bk):
                    for t in range(HTILES):
                        last = nc.tensor.transpose(ps[:, bk, t * P:(t + 1) * P], xn[:, t, k * P:(k + 1) * P],
                                                   ident[:, :])
                    return last

                pe.wait_ge(xn_ready, 1)
                for k in range(KT):
                    transposes(k, k).then_inc(job_done, 1)
                pe.wait_ge(w_split, KT)
                pe.wait_ge(sm_split, 2)
                pe.wait_ge(bkT_split, 1)

                def steps(b):
                    for hh in range(2):
                        n = 2 * b + hh
                        pe.wait_ge(xlo_ready, KT * (n + 1))
                        for name in JOBS:
                            bk = bank(hh, name)
                            dst = ps[:, bk, :]
                            free = bank_free(b, hh, name)
                            if free is not None:
                                pe.wait_ge(bank_read, free)
                            columns = {"mp": MP, "pi": PI, "ql": QL, "qs": QS, "kl": KL, "ks": KS}
                            if name in columns:
                                c = slice(columns[name] * P, (columns[name] + 1) * P)
                                for k in range(KT):
                                    last = product(nc, dst, wp_hi[:, k, c], wp_lo[:, k, c], xnT_hi[:, hh, k, :],
                                                   xnT_lo[:, hh, k, :], k == 0, k == KT - 1)
                            elif name == "ms":
                                pe.wait_ge(lo_ready, lo(n, "xp"))
                                for t in range(HTILES):
                                    c = slice(t * P, (t + 1) * P)
                                    last = product(nc, dst[:, t * MEM:(t + 1) * MEM], act_hi[:, XP, c],
                                                   act_lo[:, XP, c], bkT_hi[:, :], bkT_lo[:, :], True, True)
                            elif name in ("p1a", "p1b"):
                                c = 2 + int(name == "p1b")
                                pe.wait_ge(lo_ready, lo(n, "pin"))
                                last = product(nc, dst, sm_hi[:, c, :], sm_lo[:, c, :], act_hi[:, PIN, :],
                                               act_lo[:, PIN, :], True, True)
                            elif name == "wt":
                                wait_alone(pe, wn_ready, n + 1, pe_passed)
                                for t in range(HTILES):
                                    last = nc.tensor.transpose(ps[0:MEM, bk, t * P:(t + 1) * P], we[:, t, :],
                                                               ident[:, :])
                            elif name == "ret":
                                pe.wait_ge(lo_ready, lo(n, "wt"))
                                last = product(nc, dst, sm_hi[0:MEM, 6, :], sm_lo[0:MEM, 6, :],
                                               act_hi[0:MEM, WT, :], act_lo[0:MEM, WT, :], True, True)
                            elif name == "p2":
                                pe.wait_ge(lo_ready, lo(n, "gelu"))
                                for c in range(2):
                                    last = product(nc, dst, sm_hi[:, 4 + c, :], sm_lo[:, 4 + c, :],
                                                   gelu_hi[:, c, :], gelu_lo[:, c, :], c == 0, c == 1)
                            elif name == "mo":
                                pe.wait_ge(lo_ready, lo(n, "ret"))
                                for c, slot in enumerate((XP, RET)):
                                    last = product(nc, dst, sm_hi[:, c, :], sm_lo[:, c, :], act_hi[:, slot, :],
                                                   act_lo[:, slot, :], c == 0, c == 1)
                            elif name in ("v01", "v23"):
                                v = slice(VL * P, (VS + 1) * P)
                                for tt in range(2):
                                    t = 2 * int(name == "v23") + tt
                                    c = slice(t * P, (t + 1) * P)
                                    for k in range(KT):
                                        last = product(nc, dst[:, tt * 2 * P:(tt + 1) * 2 * P], xnT_hi[:, hh, k, c],
                                                       xnT_lo[:, hh, k, c], wp_hi[:, k, v], wp_lo[:, k, v],
                                                       k == 0, k == KT - 1)
                            else:
                                if name == "tr0":
                                    pe.wait_ge(xn_ready, n + 2)
                                last = transposes(int(name[2]), bk)
                            last.then_inc(job_done, 1)

                steps(0)
                with pe.Fori(1, B) as b:
                    steps(b)


def stage2(nc, x, w, xnT_d, kv_d, tile_d, ident, ww_hi, ww_lo, rows, pick, w2, b1, out):
    HC = CH // HTILES
    BC = 2 * CH
    GAP = 4

    with ExitStack() as ctx:
        def sb(name, shape, dt):
            return ctx.enter_context(nc.sbuf_tensor(name, shape, dt))

        def sem(name):
            return ctx.enter_context(nc.semaphore(name))

        units = sb("units", [P, 4, HALF], F32)
        xnT_hi = sb("xnT_hi", [P, KT, HALF], F32R)
        xnT_lo = sb("xnT_lo", [P, KT, HALF], F32R)
        kv_hi = sb("kv_hi", [P, 8, HALF], F32R)
        kv_lo = sb("kv_lo", [P, 8, HALF], F32R)
        tl = sb("tl", [P, 4, P], F32)
        tl_hi = sb("tl_hi", [P, 2, 4, P], F32R)
        tl_lo = sb("tl_lo", [P, 2, 4, P], F32R)
        w1 = sb("w1", [P, 2, KT, P], F32)
        w1_hi = sb("w1_hi", [P, 2, KT, P], F32R)
        w1_lo = sb("w1_lo", [P, 2, KT, P], F32R)
        w2_hi = sb("w2_hi", [P, 2, D], F32R)
        w2_lo = sb("w2_lo", [P, 2, D], F32R)
        h32 = sb("h32", [P, 2, HALF], F32)
        h_hi = sb("h_hi", [P, 2, HALF], F32R)
        h_lo = sb("h_lo", [P, 2, HALF], F32R)
        sc = sb("sc", [P, 2, S], F32)
        larger = sb("larger", [P, S // 2], F32)
        smaller = sb("smaller", [P, S // 2], F32)
        top_l = sb("top_l", [P, 8 * ROUNDS], F32)
        top_s = sb("top_s", [P, 1 + 8 * ROUNDS_S], F32)
        ranked = sb("ranked", [P, 1 + 8 * ROUNDS_S], F32)
        kth = sb("kth", [P, 1], F32)
        nms = sb("nms", [P, 2], F32)
        mxl = sb("mxl", [P, 1], F32)
        nml = sb("nml", [P, 1], F32)
        sums = sb("sums", [P, 2], F32)
        inv = sb("inv", [P, 2], F32)
        prob = sb("prob", [P, 2, S], F32)
        pT = sb("pT", [P, 2, 512], F32)
        pT_hi = sb("pT_hi", [P, S], F32R)
        pT_lo = sb("pT_lo", [P, S], F32R)
        at = sb("at", [P, 2, P], F32)
        at_hi = sb("at_hi", [P, 2, P], F32R)
        at_lo = sb("at_lo", [P, 2, P], F32R)
        mixed = sb("mixed", [P, HTILES, D], F32)
        gate = sb("gate", [P, HTILES, D], F32)
        xin = sb("xin", [P, 2, D], F32)
        scores = ctx.enter_context(nc.psum_tensor("scores", [P, S], F32))
        hid = ctx.enter_context(nc.psum_tensor("hid", [P, HALF], F32))
        o = ctx.enter_context(nc.psum_tensor("o", [P, D], F32))
        acc = ctx.enter_context(nc.psum_tensor("acc", [P, HTILES, D], F32))

        w1_in = [sem("w1_in0"), sem("w1_in1")]
        units_in = [sem(f"units_in{j}") for j in range(4)]
        xr_in = [sem("xr_in0"), sem("xr_in1")]
        tl_in = sem("tl_in")
        out_st = [sem(f"out_st{t}") for t in range(HTILES)]
        w1_h, w1_l = sem("w1_h"), sem("w1_l")
        w2_h, w2_l = sem("w2_h"), sem("w2_l")
        kv_h, kv_l = sem("kv_h"), sem("kv_l")
        xn_h, xn_l = sem("xn_h"), sem("xn_l")
        tl_h, tl_l = sem("tl_h"), sem("tl_l")
        h_h, h_l = sem("h_h"), sem("h_l")
        pT_h, pT_l = sem("pT_h"), sem("pT_l")
        at_h, at_l = sem("at_h"), sem("at_l")
        f1_done = sem("f1_done")
        f2_done = sem("f2_done")
        ss_done = sem("ss_done")
        sl_done = sem("sl_done")
        tr_done = sem("tr_done")
        pv_done = sem("pv_done")
        mix_done = sem("mix_done")
        sc_ready = sem("sc_ready")
        tanh_ready = sem("tanh_ready")
        mix_ready = sem("mix_ready")
        es_ready = sem("es_ready")
        el_ready = sem("el_ready")
        pr_ready = sem("pr_ready")
        step = sem("step")
        nms_ready = sem("nms_ready")
        nml_step = sem("nml_step")
        nml_ready = sem("nml_ready")
        masked = sem("masked")
        invs_ready = sem("invs_ready")
        invl_ready = sem("invl_ready")
        gate_ready = sem("gate_ready")
        prod_ready = sem("prod_ready")
        fin_ready = sem("fin_ready")

        sp_passed, dve_passed = sem("sp_passed"), sem("dve_passed")

        STEPS = 2 + (2 * ROUNDS - 1) + (2 * ROUNDS_S - 1) + 2

        def known_first(v, least):
            return isinstance(v, int) and v < least

        with nc.Block() as block:
            @block.sync
            def _(sp):
                def load_w1(C, c):
                    if not known_first(C, 2):
                        sp.wait_ge(w1_l, C - 1)
                    sp.dma_start(w1[:, c % 2, :, :], w["w1"].rearrange("(k p) n -> p k n", p=P)
                                 [:, :, (c % CH) * P:(c % CH + 1) * P]).then_inc(w1_in[c % 2], 16)

                def load_kv(b, u, src):
                    before = 8 * b + u - 3
                    if not known_first(before, 1):
                        wait_alone(sp, xn_l, before, sp_passed)
                    sp.dma_start(units[:, u % 4, :], kv_d[bass.ds(src, 1), :, u, :]
                                 .rearrange("a p n -> p (a n)")).then_inc(units_in[u % 4], 16)

                def load_xn(h, k, src):
                    wait_alone(sp, kv_l, 4 * h + k + 1, sp_passed)
                    sp.dma_start(units[:, k, :], xnT_d[bass.ds(src, 1), :, k, :]
                                 .rearrange("a p n -> p (a n)")).then_inc(units_in[k], 16)

                def load_tl(m, src):
                    if not known_first(m, 1):
                        wait_alone(sp, tl_l, m, sp_passed)
                    sp.dma_start(tl[:, :, :], tile_d[bass.ds(src, 1), :, :, :]
                                 .rearrange("a p s n -> p (a s) n")).then_inc(tl_in, 16)

                load_tl(0, 0)
                for u in range(4):
                    load_kv(0, u, 0)
                load_w1(0, 0)
                load_w1(1, 1)
                for k in range(KT):
                    load_xn(0, k, 0)
                load_w1(2, 2)
                load_w1(3, 3)
                for u in range(4, 8):
                    load_kv(0, u, 0)

                def load_x(m, b, T):
                    if not known_first(m, 2):
                        wait_alone(sp, fin_ready, m - 1, sp_passed)
                    sp.dma_start(xin[:, T % 2, :], x[bass.ds(b, 1), T * P:(T + 1) * P, :]
                                 .rearrange("a p n -> p (a n)")).then_inc(xr_in[T % 2], 16)

                def store(m, b, T):
                    wait_alone(sp, fin_ready, m + 1, sp_passed)
                    sp.dma_start(out[bass.ds(b, 1), T * P:(T + 1) * P, :].rearrange("a p n -> p (a n)"),
                                 gate[:, T % HTILES, :]).then_inc(out_st[T % HTILES], 16)

                def slots(b):
                    nb = (b + 1) & (B - 1)
                    for T in range(TILES):
                        m, C, t = b * TILES + T, b * BC + T * HC, T % HTILES
                        pb, pT = (b, 0) if T >= HTILES else (b - 1, HTILES)
                        pm = m - t - HTILES
                        some = not known_first(m, HTILES)
                        load_w1(C + 4, T * HC + 4)
                        load_tl(m + 1, m + 1 if T < TILES - 1 else nb * TILES)
                        if t == 2:
                            load_x(m - 2, b, T - 2)
                            load_x(m - 1, b, T - 1)
                        if T == 1:
                            load_xn(2 * b + 1, 2, 2 * b + 1)
                            load_xn(2 * b + 1, 3, 2 * b + 1)
                        if T == TILES - 1:
                            load_xn(2 * b + 2, 0, 2 * nb)
                            load_xn(2 * b + 2, 1, 2 * nb)
                        if t == 0 and some:
                            load_x(pm + 2, pb, pT + 2)
                            store(pm, pb, pT)
                        load_w1(C + 5, T * HC + 5)
                        if T == 0:
                            load_xn(2 * b + 1, 0, 2 * b + 1)
                            load_xn(2 * b + 1, 1, 2 * b + 1)
                        if t == 0 and some:
                            load_x(pm + 3, pb, pT + 3)
                            store(pm + 1, pb, pT + 1)
                        if t == 2 and some:
                            store(pm + 3, pb, pT + 3)
                        load_w1(C + 6, T * HC + 6)
                        if T == TILES - 1:
                            load_xn(2 * b + 2, 2, 2 * nb)
                            load_xn(2 * b + 2, 3, 2 * nb)
                        if t == 0 and some:
                            store(pm + 2, pb, pT + 2)
                        if t == HTILES - 1:
                            for u in range(4):
                                load_kv(b + 1, u + (0 if T < HTILES else 4), nb)
                        load_w1(C + 7, T * HC + 7)

                slots(0)
                with sp.Fori(1, B) as b:
                    slots(b)
                for T in range(HTILES, TILES):
                    m = (B - 1) * TILES + T
                    if T >= HTILES + 2:
                        load_x(m, B - 1, T)
                for T in range(HTILES, TILES):
                    store((B - 1) * TILES + T, B - 1, T)
                for t in range(HTILES):
                    sp.wait_ge(out_st[t], 16 * 2 * B)
                for j in range(2):
                    sp.wait_ge(w1_in[j], 16 * (B * BC // 2 + 2))

            @block.scalar
            def _(act):
                def hi(out_, src, ready):
                    return nc.scalar.activation(out_, src, ACT.Copy).then_inc(ready, 1)

                def split_w1(C, c):
                    act.wait_ge(w1_in[c % 2], 8 * (C - c % 2) + 16)
                    hi(w1_hi[:, c % 2, :, :], w1[:, c % 2, :, :], w1_h)

                def split_kv(g, u):
                    act.wait_ge(units_in[u % 4], 8 * (g - u % 4) + 16)
                    hi(kv_hi[:, u, :], units[:, u % 4, :], kv_h)

                def split_xn(h, k):
                    act.wait_ge(units_in[k], 32 * h + 32)
                    hi(xnT_hi[:, k, :], units[:, k, :], xn_h)

                def split_tl(m, parity):
                    act.wait_ge(tl_in, 16 * m + 16)
                    hi(tl_hi[:, parity, :, :], tl[:, :, :], tl_h)

                def sparse_scores(m, parity):
                    act.wait_ge(ss_done, m + 1)
                    if not known_first(m, 2):
                        act.wait_ge(masked, m - 1)
                    nc.scalar.activation(sc[:, parity, :], scores[:, :], ACT.Copy, scale=SCALE).then_inc(sc_ready, 1)

                def chunk(C, c, h_next):
                    act.wait_ge(f1_done, C + 1)
                    if not known_first(C, 2):
                        act.wait_ge(h_l, C - 1)
                        act.wait_ge(f2_done, C - 1)
                    bias = b1[:, c % CH:c % CH + 1]
                    nc.scalar.activation(h32[:, c % 2, :], hid[:, :], ACT.Relu, bias=bias)
                    nc.scalar.activation(h_hi[:, c % 2, :], hid[:, :], ACT.Relu, bias=bias).then_inc(h_h, 1)
                    hi(w2_hi[:, c % 2, :], w2[:, c % CH, :], w2_h)
                    if c % CH == CH - 1:
                        for k in range(KT):
                            split_xn(h_next, k)
                    split_w1(C + 2, c + 2)

                def transposed(i):
                    act.wait_ge(tr_done, i + 1)
                    for j in range(2):
                        if not known_first(i, 1):
                            act.wait_ge(pT_l, 2 * i - 1 + j)
                        c = slice(j * 512, (j + 1) * 512)
                        nc.scalar.activation(pT[:, j, :], scores[:, c], ACT.Copy)
                        nc.scalar.activation(pT_hi[:, c], scores[:, c], ACT.Copy).then_inc(pT_h, 1)

                def head_out(i, head):
                    act.wait_ge(pv_done, i + 1)
                    nc.scalar.activation(at[:, head, :], o[:, 0:P], ACT.Copy)
                    nc.scalar.activation(at_hi[:, head, :], o[:, 0:P], ACT.Copy).then_inc(at_h, 1)

                def gates(h):
                    act.wait_ge(f2_done, CH * (h + 1))
                    for t in range(HTILES):
                        if not known_first(h, 1):
                            act.wait_ge(out_st[t], 16 * h)
                        nc.scalar.activation(gate[:, t, :], acc[:, t, :], ACT.Tanh, scale=0.5).then_inc(tanh_ready, 1)

                def mix(m, t):
                    act.wait_ge(mix_done, m + 1)
                    if not known_first(m, HTILES):
                        act.wait_ge(prod_ready, m - HTILES + 1)
                    nc.scalar.activation(mixed[:, t, :], o[:, :], ACT.Copy, scale=0.5).then_inc(mix_ready, 1)

                split_tl(0, 0)
                for u in range(4):
                    split_kv(u, u)
                split_w1(0, 0)
                split_w1(1, 1)
                for k in range(KT):
                    split_xn(0, k)

                def sparse_end(m):
                    act.wait_ge(invs_ready, m + 1)
                    nc.scalar.activation(prob[:, 1, :], prob[:, 1, :], ACT.Copy, scale=inv[:, 1:2]).then_inc(pr_ready, 1)
                    transposed(2 * m + 1)

                def slots(b):
                    for T in range(TILES):
                        m, C, c = b * TILES + T, b * BC + T * HC, T * HC
                        h = 2 * b + T // HTILES
                        some = not known_first(m, 1)
                        sparse_scores(m, T % 2)
                        if T % HTILES == 0 and some:
                            gates(h - 1)
                        chunk(C, c, h + 1)
                        if some:
                            head_out(2 * m - 2, 0)
                        if T == 1:
                            split_kv(8 * b + GAP + 2, U_VS)
                            split_kv(8 * b + GAP + 3, U_VS + 1)
                        if T == TILES - 1:
                            split_kv(8 * b + GAP + 4, U_KS)
                            split_kv(8 * b + GAP + 5, U_KS + 1)
                        if some:
                            sparse_end(m - 1)
                        chunk(C + 1, c + 1, h + 1)
                        act.wait_ge(nms_ready, m + 1)
                        nc.scalar.activation(prob[:, 1, :], sc[:, T % 2, :], ACT.Exp, bias=nms[:, T % 2:T % 2 + 1])\
                            .then_inc(es_ready, 1)
                        if T == 0:
                            split_kv(8 * b + GAP, U_VL)
                            split_kv(8 * b + GAP + 1, U_VL + 1)
                        if some:
                            head_out(2 * m - 1, 1)
                        act.wait_ge(nml_ready, m + 1)
                        nc.scalar.activation(prob[:, 0, :], scores[:, :], ACT.Exp, bias=nml[:, :], scale=SCALE,
                                             accum_out=sums[:, 0:1]).then_inc(el_ready, 1)
                        act.wait_ge(invl_ready, m + 1)
                        nc.scalar.activation(prob[:, 0, :], prob[:, 0, :], ACT.Copy, scale=inv[:, 0:1])\
                            .then_inc(pr_ready, 1)
                        chunk(C + 2, c + 2, h + 1)
                        if T == TILES - 1:
                            split_kv(8 * b + GAP + 6, U_KL)
                            split_kv(8 * b + GAP + 7, U_KL + 1)
                        if some:
                            mix(m - 1, (T - 1) % HTILES)
                        split_tl(m + 1, (T + 1) % 2)
                        transposed(2 * m)
                        chunk(C + 3, c + 3, h + 1)

                slots(0)
                with act.Fori(1, B) as b:
                    slots(b)
                head_out(2 * B * TILES - 2, 0)
                gates(2 * B - 1)
                sparse_end(B * TILES - 1)
                head_out(2 * B * TILES - 1, 1)
                mix(B * TILES - 1, HTILES - 1)

            @block.gpsimd
            def _(pool):
                def lo(out_, value, hi_, ready):
                    return nc.gpsimd.tensor_tensor(out_, value, hi_.bitcast(F32), ALU.subtract).then_inc(ready, 1)

                def split_w1(C, c):
                    pool.wait_ge(w1_h, C + 1)
                    lo(w1_lo[:, c % 2, :, :], w1[:, c % 2, :, :], w1_hi[:, c % 2, :, :], w1_l)

                def split_kv(g, u):
                    pool.wait_ge(kv_h, g + 1)
                    lo(kv_lo[:, u, :], units[:, u % 4, :], kv_hi[:, u, :], kv_l)

                def split_tl(m, parity):
                    pool.wait_ge(tl_h, m + 1)
                    lo(tl_lo[:, parity, :, :], tl[:, :, :], tl_hi[:, parity, :, :], tl_l)

                def chunk(C, c):
                    pool.wait_ge(h_h, C + 1)
                    lo(h_lo[:, c % 2, :], h32[:, c % 2, :], h_hi[:, c % 2, :], h_l)
                    pool.wait_ge(w2_h, C + 1)
                    lo(w2_lo[:, c % 2, :], w2[:, c % CH, :], w2_hi[:, c % 2, :], w2_l)
                    split_w1(C + 2, c + 2)

                def transposed(i):
                    for j in range(2):
                        pool.wait_ge(pT_h, 2 * i + j + 1)
                        lo(pT_lo[:, j * 512:(j + 1) * 512], pT[:, j, :], pT_hi[:, j * 512:(j + 1) * 512], pT_l)

                def head_out(i, head):
                    pool.wait_ge(at_h, i + 1)
                    lo(at_lo[:, head, :], at[:, head, :], at_hi[:, head, :], at_l)

                def residual(m, T):
                    t = T % HTILES
                    pool.wait_ge(gate_ready, m + 1)
                    pool.wait_ge(mix_ready, m + 1)
                    nc.gpsimd.tensor_tensor(gate[:, t, :], gate[:, t, :], mixed[:, t, :], ALU.mult)\
                        .then_inc(prod_ready, 1)
                    pool.wait_ge(prod_ready, m + 1)
                    pool.wait_ge(xr_in[T % 2], 8 * (m - T % 2) + 16)
                    nc.gpsimd.tensor_tensor(gate[:, t, :], gate[:, t, :], xin[:, T % 2, :], ALU.add)\
                        .then_inc(fin_ready, 1)

                split_tl(0, 0)
                for u in range(4):
                    split_kv(u, u)
                split_w1(0, 0)
                split_w1(1, 1)

                def slots(b):
                    for T in range(TILES):
                        m, C, c = b * TILES + T, b * BC + T * HC, T * HC
                        t = T % HTILES
                        some = not known_first(m, 1)
                        finish = t == 0 and not known_first(m, HTILES)
                        pm, pT = m - HTILES, (T - HTILES) % TILES
                        chunk(C, c)
                        if some:
                            head_out(2 * m - 2, 0)
                        if T == 1:
                            split_kv(8 * b + GAP + 2, U_VS)
                            split_kv(8 * b + GAP + 3, U_VS + 1)
                        if T == TILES - 1:
                            split_kv(8 * b + GAP + 4, U_KS)
                            split_kv(8 * b + GAP + 5, U_KS + 1)
                        if finish:
                            residual(pm, pT)
                        if some:
                            transposed(2 * m - 1)
                        chunk(C + 1, c + 1)
                        if T == 0:
                            split_kv(8 * b + GAP, U_VL)
                            split_kv(8 * b + GAP + 1, U_VL + 1)
                        if finish:
                            residual(pm + 1, pT + 1)
                        if some:
                            head_out(2 * m - 1, 1)
                        chunk(C + 2, c + 2)
                        if T == TILES - 1:
                            split_kv(8 * b + GAP + 6, U_KL)
                            split_kv(8 * b + GAP + 7, U_KL + 1)
                        split_tl(m + 1, (T + 1) % 2)
                        if finish:
                            residual(pm + 2, pT + 2)
                        if t == 1 and not known_first(m, HTILES):
                            residual(m - 2, (T - 2) % TILES)
                        transposed(2 * m)
                        chunk(C + 3, c + 3)

                slots(0)
                with pool.Fori(1, B) as b:
                    slots(b)
                head_out(2 * B * TILES - 2, 0)
                transposed(2 * B * TILES - 1)
                head_out(2 * B * TILES - 1, 1)
                for T in range(HTILES, TILES):
                    residual((B - 1) * TILES + T, T)

            @block.vector
            def _(dve):
                def apply_threshold(m, T):
                    dve.wait_ge(step, 1 + STEPS * (T + 1))
                    dve.wait_ge(es_ready, m + 1)
                    nc.vector.scalar_tensor_tensor(out=prob[:, 1, :], in0=sc[:, T % 2, :], scalar=kth[:, :],
                                                   in1=prob[:, 1, :], op0=ALU.is_ge, op1=ALU.mult,
                                                   accum_out=sums[:, 1:2]).then_inc(masked, 1)
                    dve.wait_ge(masked, m + 1)
                    nc.vector.reciprocal(inv[:, 1:2], sums[:, 1:2]).then_inc(invs_ready, 1)

                def gates(h):
                    for t in range(HTILES):
                        dve.wait_ge(tanh_ready, HTILES * h + t + 1)
                        nc.vector.scalar_tensor_tensor(out=gate[:, t, :], in0=gate[:, t, :], scalar=1.0,
                                                       in1=acc[:, t, :], op0=ALU.add, op1=ALU.mult)\
                            .then_inc(gate_ready, 1)

                def full_max(m):
                    dve.wait_ge(sl_done, m + 1)
                    nc.vector.tensor_reduce(mxl[:, :], scores[:, :], AX_X, ALU.max).then_inc(nml_step, 1)
                    dve.wait_ge(nml_step, m + 1)
                    nc.vector.tensor_scalar(nml[:, :], mxl[:, :], -SCALE, None, ALU.mult).then_inc(nml_ready, 1)

                def full_inverse(m):
                    dve.wait_ge(el_ready, m + 1)
                    nc.vector.reciprocal(inv[:, 0:1], sums[:, 0:1]).then_inc(invl_ready, 1)

                def search(m, T, b):
                    done = [1 + STEPS * T]

                    def count(ins):
                        ins.then_inc(step, 1)
                        done[0] += 1
                        return done[0]

                    wait_alone(dve, sc_ready, m + 1, dve_passed)
                    lo_half, hi_half = sc[:, T % 2, 0:S // 2], sc[:, T % 2, S // 2:S]
                    l_step = count(nc.vector.tensor_tensor(larger[:, :], lo_half, hi_half, ALU.max))
                    s_step = count(nc.vector.tensor_tensor(smaller[:, :], lo_half, hi_half, ALU.min))
                    for r in range(ROUNDS):
                        own = slice(8 * r, 8 * r + 8)
                        dve.wait_ge(step, l_step)
                        l_step = count(nc.vector.max(top_l[:, own], larger[:, :]))
                        if r < ROUNDS_S:
                            own_s = slice(1 + 8 * r, 9 + 8 * r)
                            dve.wait_ge(step, s_step)
                            s_step = count(nc.vector.max(top_s[:, own_s], smaller[:, :]))
                        if r == 1:
                            gates_of_half(m, T, b)
                        if r == 5:
                            full_max(m)
                        if r == 6:
                            full_inverse(m)
                        if r < ROUNDS - 1:
                            dve.wait_ge(step, l_step)
                            l_step = count(nc.vector.match_replace(larger[:, :], top_l[:, own], larger[:, :], LOWEST))
                        if r < ROUNDS_S - 1:
                            dve.wait_ge(step, s_step)
                            s_step = count(nc.vector.match_replace(smaller[:, :], top_s[:, own_s], smaller[:, :],
                                                                   LOWEST))
                        if r == 0:
                            nc.vector.tensor_scalar(nms[:, T % 2:T % 2 + 1], top_l[:, 0:1], -1.0, None, ALU.mult)\
                                .then_inc(nms_ready, 1)
                    n = 1 + 8 * ROUNDS_S
                    dve.wait_ge(step, l_step)
                    merged = count(nc.vector.tensor_tensor(ranked[:, :], top_l[:, TOPK - n:TOPK], top_s[:, ::-1],
                                                           ALU.min))
                    dve.wait_ge(step, merged)
                    count(nc.vector.tensor_reduce(kth[:, :], ranked[:, :], AX_X, ALU.max))
                    assert done[0] == 1 + STEPS * (T + 1)

                def gates_of_half(m, T, b):
                    if T % HTILES == 0 and not known_first(m, 1):
                        gates(2 * b + T // HTILES - 1)

                def split_xn(h):
                    for k in range(KT):
                        dve.wait_ge(xn_h, KT * h + k + 1)
                        nc.vector.tensor_tensor(xnT_lo[:, k, :], units[:, k, :], xnT_hi[:, k, :].bitcast(F32),
                                                ALU.subtract).then_inc(xn_l, 1)

                split_xn(0)

                def slots(b):
                    for T in range(TILES):
                        m = b * TILES + T
                        if not known_first(m, 1):
                            apply_threshold(m - 1, (T - 1) % TILES)
                        if T == 0:
                            if not known_first(m, 1):
                                nc.vector.sem_clear(step)
                            nc.vector.memset(top_s[:, 0:1], HIGHEST).then_inc(step, 1)
                            dve.wait_ge(step, 1)
                        search(m, T, b)
                        if T % HTILES == HTILES - 1:
                            split_xn(2 * b + 1 + T // HTILES)

                slots(0)
                with dve.Fori(1, B) as b:
                    slots(b)
                apply_threshold(B * TILES - 1, TILES - 1)
                gates(2 * B - 1)

            @block.tensor
            def _(pe):
                def f1(C, c, h):
                    pe.wait_ge(w1_l, C + 1)
                    if not known_first(C, 1):
                        pe.wait_ge(h_h, C)
                    for k in range(KT):
                        if c % CH == 0:
                            pe.wait_ge(xn_l, KT * h + k + 1)
                        last = product(nc, hid[:, :], w1_hi[:, c % 2, k, :], w1_lo[:, c % 2, k, :],
                                       xnT_hi[:, k, :], xnT_lo[:, k, :], k == 0, k == KT - 1)
                    last.then_inc(f1_done, 1)

                def f2(C, c, h):
                    pe.wait_ge(h_l, C + 1)
                    pe.wait_ge(w2_l, C + 1)
                    start = c % CH == 0
                    if start and not known_first(C, 1):
                        pe.wait_ge(gate_ready, HTILES * h)
                    for t in range(HTILES):
                        last = product(nc, acc[:, t, :], h_hi[:, c % 2, t * P:(t + 1) * P],
                                       h_lo[:, c % 2, t * P:(t + 1) * P], w2_hi[:, c % 2, :], w2_lo[:, c % 2, :],
                                       start, False)
                        if c % CH == CH - 1:
                            last = nc.tensor.matmul(acc[:, t, :], pick[:, 1, :], rows[:, :], start=False, stop=True)
                    last.then_inc(f2_done, 1)

                def head_scores(parity, slot, unit, done):
                    for j in range(2):
                        last = product(nc, scores[:, j * 512:(j + 1) * 512], tl_hi[:, parity, slot, :],
                                       tl_lo[:, parity, slot, :], kv_hi[:, unit + j, :], kv_lo[:, unit + j, :],
                                       True, True)
                    last.then_inc(done, 1)

                def transposes(i, head):
                    pe.wait_ge(pr_ready, i + 1)
                    for j in range(TILES):
                        last = nc.tensor.transpose(scores[:, j * P:(j + 1) * P], prob[:, head, j * P:(j + 1) * P],
                                                   ident[:, :])
                    last.then_inc(tr_done, 1)

                def head_out(i, unit):
                    pe.wait_ge(pT_l, 2 * i + 2)
                    for j in range(TILES):
                        u, c = unit + j // HTILES, slice((j % HTILES) * P, (j % HTILES + 1) * P)
                        last = product(nc, o[:, 0:P], kv_hi[:, u, c], kv_lo[:, u, c], pT_hi[:, j * P:(j + 1) * P],
                                       pT_lo[:, j * P:(j + 1) * P], j == 0, j == TILES - 1)
                    last.then_inc(pv_done, 1)

                def sparse_head_out(m, b_kv):
                    pe.wait_ge(at_h, 2 * m + 1)
                    pe.wait_ge(kv_l, b_kv)
                    head_out(2 * m + 1, U_VS)

                def mix(m, parity):
                    pe.wait_ge(at_l, 2 * m + 2)
                    for j in range(2):
                        product(nc, o[:, :], at_hi[:, j, :], at_lo[:, j, :], ww_hi[:, j, :], ww_lo[:, j, :],
                                j == 0, False)
                    for j in (T_MEM, T_PRED):
                        product(nc, o[:, :], tl_hi[:, parity, j, :], tl_lo[:, parity, j, :], ww_hi[:, j, :],
                                ww_lo[:, j, :], False, False)
                    nc.tensor.matmul(o[:, :], pick[:, 0, :], rows[:, :], start=False, stop=True)\
                        .then_inc(mix_done, 1)

                def sparse_scores(m, parity, kv_count):
                    pe.wait_ge(tl_l, m + 1)
                    if kv_count is not None:
                        pe.wait_ge(kv_l, kv_count)
                    head_scores(parity, T_QS, U_KS, ss_done)

                def slots(b):
                    for T in range(TILES):
                        m, C, c = b * TILES + T, b * BC + T * HC, T * HC
                        h, t = 2 * b + T // HTILES, T % HTILES
                        some = not known_first(m, 1)
                        if some:
                            pe.wait_ge(pT_h, 4 * m - 2)
                        sparse_scores(m, T % 2, 8 * b + 2 if T == 0 else None)
                        f1(C, c, h)
                        if some:
                            if not known_first(m, 2):
                                pe.wait_ge(mix_ready, m - 1)
                            head_out(2 * m - 2, U_VL)
                        if t > 0:
                            f2(C - 1, c - 1, h)
                        pe.wait_ge(sc_ready, m + 1)
                        if some:
                            transposes(2 * m - 1, 1)
                        f1(C + 1, c + 1, h)
                        if some:
                            pe.wait_ge(pT_h, 4 * m)
                        if T == 0:
                            pe.wait_ge(kv_l, 8 * b + GAP)
                        head_scores(T % 2, T_QL, U_KL, sl_done)
                        f2(C, c, h)
                        if some:
                            sparse_head_out(m - 1, 8 * b + GAP + (4 if T > 0 else 0))
                        f1(C + 2, c + 2, h)
                        f2(C + 1, c + 1, h)
                        if some:
                            mix(m - 1, (T + 1) % 2)
                        transposes(2 * m, 0)
                        f1(C + 3, c + 3, h)
                        f2(C + 2, c + 2, h)
                        if t == HTILES - 1:
                            f2(C + 3, c + 3, h)

                slots(0)
                with pe.Fori(1, B) as b:
                    slots(b)
                m = B * TILES - 1
                pe.wait_ge(mix_ready, m)
                head_out(2 * m, U_VL)
                pe.wait_ge(pT_h, 4 * m + 2)
                transposes(2 * m + 1, 1)
                sparse_head_out(m, 8 * B + GAP)
                mix(m, m % 2)


def program(nc, ins, out):
    names = {n.removeprefix("L0_attn_").removeprefix("L0_ffn_"): a for n, a in ins.items()}
    build(nc, names["x"], names, out)


_OUT = ((B, S, D), "float32")
_ORDER = ["L0_attn_x", "L0_attn_local_qkv_w", "L0_attn_sparse_qkv_w", "L0_attn_memory_bank",
          "L0_attn_memory_proj_w", "L0_attn_mem_out_w", "L0_attn_mem_out_b", "L0_attn_pred_in_w",
          "L0_attn_pred_in_b", "L0_attn_pred1_w", "L0_attn_pred1_b", "L0_attn_pred2_w", "L0_attn_pred2_b",
          "L0_attn_warboss_w", "L0_attn_warboss_b", "L0_ffn_w1", "L0_ffn_b1", "L0_ffn_w2", "L0_ffn_b2"]


def kernel(**inputs):
    import numpy as _np
    import concourse.bacc as _bacc
    from concourse import mybir as _mybir
    from concourse.bass_utils import run_bass_kernel_spmd as _run

    nc = _bacc.Bacc("TRN2", target_bir_lowering=False, num_devices=1)
    arrays, args = {}, {}
    for name in _ORDER:
        a = _np.ascontiguousarray(inputs[name])
        arrays[f"in_{name}"] = a
        args[name] = nc.dram_tensor(f"in_{name}", a.shape, _mybir.dt.from_np(a.dtype), kind="ExternalInput").ap()
    shape, dtype = _OUT
    out = nc.dram_tensor("out_0", shape, _mybir.dt.from_np(_np.dtype(dtype)), kind="ExternalOutput").ap()
    program(nc, args, out)
    r = _run(nc, [arrays], core_ids=[0])
    return r.results[0]["out_0"]
```

```python
from contextlib import ExitStack

import concourse.bass as bass
from concourse import mybir

F32 = mybir.dt.float32
F32R = mybir.dt.float32r
I32 = mybir.dt.int32
ALU = mybir.AluOpType
ACT = mybir.ActivationFunctionType
AX_X = mybir.AxisListType.X

P = 128
B, S, D = 8, 1024, 512
HD, MEM = 128, 64
WIDTH = 2048
KT = D // P
HALF = 512
TILES = S // P
HTILES = HALF // P
CH = WIDTH // P
TOPK = max(1, int(S * 0.1))
ROUNDS = (TOPK + 7) // 8
ROUNDS_S = (TOPK // 2 + 7) // 8
SCALE = HD ** -0.5
EPS = 1e-5
LOWEST, HIGHEST = -3.0e38, 3.0e38
RSQRT_SEED = float(0x5F3759DF)
NEWTON = 3
LO_ROW = 32

MP, PI, QL, QS, KL, KS, VL, VS = range(8)
JOBS = ["mp", "pi", "ql", "ms", "p1a", "p1b", "qs", "wt", "kl", "ks", "ret", "p2",
        "tr0", "tr1", "tr2", "tr3", "mo", "v01", "v23"]
NJ = len(JOBS)
BANKS = 8
U_KS, U_KL, U_VL, U_VS = 0, 2, 4, 6
T_QL, T_QS, T_MEM, T_PRED = range(4)


def wait_alone(eng, sem, value, passed):
    eng.wait_ge(sem, value)
    eng.sem_inc(passed, 1)


def product(nc, out, w_hi, w_lo, x_hi, x_lo, first, last):
    nc.tensor.matmul(out, w_hi, x_hi, start=first, stop=False)
    nc.tensor.matmul(out, w_hi, x_lo, start=False, stop=False)
    return nc.tensor.matmul(out, w_lo, x_hi, start=False, stop=last)


def build(nc, x, w, out):
    xnT_d = nc.dram_tensor("xnT_scratch", [2 * B, P, KT, HALF], F32)
    kv_d = nc.dram_tensor("kv_scratch", [B, P, 8, HALF], F32)
    tile_d = nc.dram_tensor("tile_scratch", [B * TILES, P, 4, P], F32)
    with ExitStack() as outer:
        def sb(name, shape, dt):
            return outer.enter_context(nc.sbuf_tensor(name, shape, dt))

        ident = sb("ident", [P, P], F32)
        ww_hi = sb("ww_hi", [P, KT, D], F32R)
        ww_lo = sb("ww_lo", [P, KT, D], F32R)
        rows = sb("rows", [P, D], F32R)
        pick = sb("pick", [P, P], F32R)
        half_bias = sb("half_bias", [P, D], F32)
        w2 = sb("w2", [P, CH, D], F32)
        b1 = sb("b1", [P, CH], F32)
        stage1(nc, x, w, xnT_d, kv_d, tile_d, ident, ww_hi, ww_lo, rows, pick, half_bias, w2, b1)
        stage2(nc, x, w, xnT_d, kv_d, tile_d, ident, ww_hi, ww_lo, rows, pick, half_bias, w2, b1, out)


def stage1(nc, x, w, xnT_d, kv_d, tile_d, ident, ww_hi, ww_lo, rows, pick, half_bias, w2, b1):
    XP, PIN, WT, RET = range(4)
    LO = ["xp", "pin", "wt", "gelu", "ret"]
    KV_SLOT = {"ks": 0, "kl": 1}
    PER = 2 * NJ
    SM_LOADS = 9
    CONSTS = 7

    with ExitStack() as ctx:
        def sb(name, shape, dt):
            return ctx.enter_context(nc.sbuf_tensor(name, shape, dt))

        def sem(name):
            return ctx.enter_context(nc.semaphore(name))

        wp_hi = sb("wp_hi", [P, KT, 8 * P], F32R)
        wp_lo = sb("wp_lo", [P, KT, 8 * P], F32R)
        staged = w2[:, :, :].rearrange("p c n -> p (c n)")
        wp = staged[:, 0:KT * 8 * P].rearrange("p (k n) -> p k n", k=KT)
        ww = staged[:, KT * 8 * P:KT * 8 * P + KT * D].rearrange("p (k n) -> p k n", k=KT)
        sm = sb("sm", [P, 7, P], F32)
        sm_hi = sb("sm_hi", [P, 7, P], F32R)
        sm_lo = sb("sm_lo", [P, 7, P], F32R)
        bkT = sb("bkT", [P, MEM], F32)
        bkT_s = sb("bkT_s", [P, 2, MEM], F32R)
        pick32 = sb("pick32", [P, P], F32)
        rows32 = sb("rows32", [P, D], F32)
        b_pi = sb("b_pi", [P, 1], F32)
        b_p1 = sb("b_p1", [P, 2], F32)
        b_p2 = sb("b_p2", [P, 1], F32)
        b_mo = sb("b_mo", [P, 1], F32)
        xin = sb("xin1", [P, HTILES, D], F32)
        stats = sb("stats", [P, HTILES, 6], F32)
        mv = sb("mv", [P, HTILES, 2], F32)
        var = sb("var", [P, HTILES], F32)
        rstd = sb("rstd", [P, HTILES], F32)
        nt = sb("nt", [P, HTILES], F32)
        xn = sb("xn", [P, HTILES, D], F32)
        xnT = sb("xnT1", [P, KT, HALF], F32)
        xnT_hi = sb("xnT1_hi", [P, 2, KT, HALF], F32R)
        xnT_lo = sb("xnT1_lo", [P, 2, KT, HALF], F32R)
        act32 = sb("act32", [P, 2, HALF], F32)
        act_hi = sb("act_hi", [P, 4, HALF], F32R)
        act_lo = sb("act_lo", [P, 4, HALF], F32R)
        gelu = sb("gelu", [P, 2, HALF], F32)
        gelu_hi = sb("gelu_hi", [P, 2, HALF], F32R)
        gelu_lo = sb("gelu_lo", [P, 2, HALF], F32R)
        nmx = sb("nmx", [P, HTILES], F32)
        esum = sb("esum", [P, HTILES], F32)
        mscore = sb("mscore", [P, HTILES, MEM], F32)
        einv = sb("einv", [P, HTILES], F32)
        we = sb("we", [P, HTILES, MEM], F32)
        tiles_out = sb("tiles_out", [P, HTILES, 4, P], F32)
        kv_out = sb("kv_out", [P, 4, HALF], F32)
        ps = ctx.enter_context(nc.psum_tensor("ps1", [P, BANKS, 512], F32))

        mp_in = sem("mp_in")
        w_in = [sem(f"w_in{k}") for k in range(KT)]
        ww_in = sem("ww_in")
        sm_in = sem("sm_in")
        rows_in = sem("rows_in")
        w2_in = sem("w2_in")
        consts = sem("consts")
        w_h = sem("w_h")
        w_split = sem("w_split")
        rows_h = sem("rows_h")
        sm_split = sem("sm_split")
        bkT_ps = sem("bkT_ps")
        bkT_out = sem("bkT_out")
        bkT_split = sem("bkT_split")
        x_in = sem("x_in")
        ln_step = sem("ln_step")
        xn_ready = sem("xn_ready")
        job_done = sem("job_done")
        bank_read = sem("bank_read")
        lo_ready = sem("lo_ready")
        ghi_ready = sem("ghi_ready")
        xlo_ready = sem("xlo_ready")
        ms_step = sem("ms_step")
        max_ready = sem("max_ready")
        inv_ready = sem("inv_ready")
        wn_ready = sem("wn_ready")
        tiles_st = sem("tiles_st")
        kv_st = sem("kv_st")
        xnT_st = sem("xnT_st")
        sp_passed, pe_passed = sem("sp1_passed"), sem("pe_passed")

        def done(n, name):
            return KT + n * NJ + JOBS.index(name) + 1

        def bank(hh, name):
            return (KT + hh * NJ + JOBS.index(name)) % BANKS

        def bank_free(b, hh, name):
            p = hh * NJ + JOBS.index(name)
            own = [q for q in range(-KT, p) if (q - p) % BANKS == 0]
            if isinstance(b, int):
                return KT + own[-1] + 1 if own else None
            near = max(q for q in range(p - BANKS - PER, p) if
                       (q >= 0 and (q - p) % BANKS == 0) or (q < 0 and (q + PER - p) % BANKS == 0))
            return KT + b * PER + near + 1

        def lo(n, name):
            return n * len(LO) + LO.index(name) + 1

        def first(n):
            return isinstance(n, int) and n == 0

        with nc.Block() as block:
            @block.sync
            def _(sp):
                sp.dma_start(xin[:, :, :], x[0, 0:HALF, :].rearrange("(t p) d -> p t d", p=P)).then_inc(x_in, 16)
                for m, name in ((MP, "memory_proj_w"), (PI, "pred_in_w")):
                    sp.dma_start(wp[:, :, m * P:(m + 1) * P], w[name].rearrange("(k p) n -> p k n", p=P))\
                        .then_inc(mp_in, 16)
                for k in range(KT):
                    pairs = wp[:, k, 2 * P:8 * P].rearrange("p (i h n) -> p i h n", h=2, n=P)
                    for head, weights in enumerate((w["local_qkv_w"], w["sparse_qkv_w"])):
                        sp.dma_start(pairs[:, :, head, :],
                                     weights[k * P:(k + 1) * P, :].rearrange("p (i n) -> p i n", n=P))\
                            .then_inc(w_in[k], 16)

                def column(name):
                    return w[name].rearrange("(p a) -> p a", a=1)

                sp.dma_start(sm[:, 0:2, :], w["mem_out_w"].rearrange("(k p) n -> p k n", p=P)).then_inc(sm_in, 16)
                sp.dma_start(sm[:, 2:4, :], w["pred1_w"].rearrange("p (k n) -> p k n", k=2)).then_inc(sm_in, 16)
                sp.dma_start(sm[:, 4:6, :], w["pred2_w"].rearrange("(k p) n -> p k n", p=P)).then_inc(sm_in, 16)
                sp.dma_start(sm[0:MEM, 6, :], w["memory_bank"]).then_inc(sm_in, 16)
                sp.dma_start(b_pi[:, :], column("pred_in_b")).then_inc(sm_in, 16)
                sp.dma_start(b_p2[:, :], column("pred2_b")).then_inc(sm_in, 16)
                sp.dma_start(b_mo[:, :], column("mem_out_b")).then_inc(sm_in, 16)
                with nc.allow_non_contiguous_dma(reason="biases by column"):
                    sp.dma_start(b_p1[:, :], w["pred1_b"].rearrange("(k p) -> p k", p=P)).then_inc(sm_in, 16)
                    sp.dma_start(b1[:, :], w["b1"].rearrange("(k p) -> p k", p=P)).then_inc(sm_in, 16)
                sp.wait_ge(consts, 1)
                for row in (0, LO_ROW):
                    sp.dma_start(rows32[row:row + 1, :], w["b2"].rearrange("(a n) -> a n", a=1)).then_inc(rows_in, 16)
                sp.dma_start(half_bias[:, :], w["warboss_b"].partition_broadcast(P)).then_inc(rows_in, 16)
                sp.dma_start(ww[:, :, :], w["warboss_w"].rearrange("(k p) n -> p k n", p=P)).then_inc(ww_in, 16)
                sp.wait_ge(xn_ready, 1)
                sp.dma_start(xin[:, :, :], x[0, HALF:S, :].rearrange("(t p) d -> p t d", p=P)).then_inc(x_in, 16)
                sp.wait_ge(w_split, 2 * KT)
                sp.dma_start(w2[:, :, :], w["w2"].rearrange("(c p) n -> p c n", p=P)).then_inc(w2_in, 16)

                def steps(b):
                    for hh in range(2):
                        n = 2 * b + hh
                        nb = (b + 1) & (B - 1)
                        wait_alone(sp, xn_ready, n + 2, sp_passed)
                        sp.dma_start(xin[:, :, :],
                                     x[bass.ds(nb, 1), hh * HALF:(hh + 1) * HALF, :]
                                     .rearrange("a (t p) d -> p (a t) d", p=P)).then_inc(x_in, 16)
                        sp.wait_ge(bank_read, KT if first(n) else done(n - 1, "tr3"))
                        sp.dma_start(xnT_d[bass.ds(n, 1), :, :, :].rearrange("a p k n -> p (a k) n"),
                                     xnT[:, :, :]).then_inc(xnT_st, 16)
                        def store_kv(first_slot):
                            own = slice(first_slot, first_slot + 2)
                            sp.dma_start(kv_d[bass.ds(b, 1), :, :, :]
                                         .rearrange("a p (u h) n -> p (a u) h n", h=2)[:, own, hh, :],
                                         kv_out[:, own, :]).then_inc(kv_st, 16)

                        wait_alone(sp, bank_read, done(n, "ks"), sp_passed)
                        store_kv(0)
                        sp.wait_ge(bank_read, done(n, "mo"))
                        sp.dma_start(tile_d[bass.ds(n * HTILES, HTILES), :, :, :].rearrange("t p s n -> p t (s n)"),
                                     tiles_out[:, :, :, :].rearrange("p t s n -> p t (s n)")).then_inc(tiles_st, 16)
                        wait_alone(sp, bank_read, done(n, "v23"), sp_passed)
                        store_kv(2)

                steps(0)
                with sp.Fori(1, B) as b:
                    steps(b)
                sp.wait_ge(xnT_st, 16 * 2 * B)
                sp.wait_ge(kv_st, 16 * 4 * B)
                sp.wait_ge(tiles_st, 16 * 2 * B)
                sp.wait_ge(w2_in, 16)

            @block.gpsimd
            def _(pool):
                pool.memset(rows32[:, :], 0.0).then_inc(consts, 1)
                pool.wait_ge(consts, 1)
                pool.memset(sm[MEM:P, 6, :], 0.0).then_inc(consts, 1)
                pool.wait_ge(consts, 2)
                pool.memset(ident[:, :], 0.0).then_inc(consts, 1)
                pool.wait_ge(consts, 3)
                pool.memset(pick32[:, :], 0.0).then_inc(consts, 1)
                pool.wait_ge(consts, 4)
                pool.affine_select(out=ident[:, :], in_=ident[:, :], compare_op=ALU.not_equal, fill=1.0,
                                   base=0, pattern=[[-1, P]], channel_multiplier=1).then_inc(consts, 1)
                for i, row in enumerate((0, LO_ROW)):
                    pool.wait_ge(consts, 5 + i)
                    pool.affine_select(out=pick32[:, :], in_=pick32[:, :], compare_op=ALU.not_equal, fill=1.0,
                                       base=-row, pattern=[[0, P]], channel_multiplier=1).then_inc(consts, 1)
                for k in range(2 * KT):
                    pool.wait_ge(w_h, k + 1)
                    lo_, src, hi = ((wp_lo[:, k, :], wp[:, k, :], wp_hi[:, k, :]) if k < KT else
                                    (ww_lo[:, k - KT, :], ww[:, k - KT, :], ww_hi[:, k - KT, :]))
                    pool.tensor_tensor(lo_, src, hi.bitcast(F32), ALU.subtract).then_inc(w_split, 1)

            @block.scalar
            def _(act):
                act.wait_ge(mp_in, 32)
                for k in range(KT):
                    act.wait_ge(w_in[k], 32)
                    nc.scalar.activation(wp_hi[:, k, :], wp[:, k, :], ACT.Copy).then_inc(w_h, 1)
                act.wait_ge(sm_in, 16 * SM_LOADS)

                for k in range(KT):
                    act.wait_ge(job_done, k + 1)
                    nc.scalar.activation(xnT[:, k, :], ps[:, k, :], ACT.Copy)
                    nc.scalar.activation(xnT_hi[:, 0, k, :], ps[:, k, :], ACT.Copy).then_inc(bank_read, 1)
                act.wait_ge(bkT_ps, 1)
                nc.scalar.activation(bkT[:, :], ps[:, BANKS - 1, 0:MEM], ACT.Copy)
                nc.scalar.activation(bkT_s[:, 0, :], ps[:, BANKS - 1, 0:MEM], ACT.Copy).then_inc(bkT_out, 1)
                act.wait_ge(ww_in, 16)
                for k in range(KT):
                    nc.scalar.activation(ww_hi[:, k, :], ww[:, k, :], ACT.Copy).then_inc(w_h, 1)

                def steps(b):
                    for hh in range(2):
                        n = 2 * b + hh
                        for name in JOBS:
                            src = ps[:, bank(hh, name), :]
                            act.wait_ge(job_done, done(n, name))
                            if name == "mp":
                                nc.scalar.activation(act32[:, XP, :], src, ACT.Copy)
                                last = nc.scalar.activation(act_hi[:, XP, :], src, ACT.Copy)
                            elif name == "pi":
                                nc.scalar.activation(act32[:, PIN, :], src, ACT.Identity, bias=b_pi[:, :])
                                last = nc.scalar.activation(act_hi[:, PIN, :], src, ACT.Identity, bias=b_pi[:, :])
                            elif name == "ret":
                                nc.scalar.activation(act32[:, RET % 2, :], src, ACT.Copy)
                                last = nc.scalar.activation(act_hi[:, RET, :], src, ACT.Copy)
                            elif name == "wt":
                                src = ps[0:MEM, bank(hh, name), :]
                                nc.scalar.activation(act32[0:MEM, WT % 2, :], src, ACT.Copy)
                                last = nc.scalar.activation(act_hi[0:MEM, WT, :], src, ACT.Copy)
                            elif name == "ms":
                                act.wait_ge(max_ready, n + 1)
                                for t in range(HTILES):
                                    last = nc.scalar.activation(we[:, t, :], mscore[:, t, :], ACT.Exp,
                                                                bias=nmx[:, t:t + 1], accum_out=esum[:, t:t + 1])
                            elif name in ("p1a", "p1b"):
                                c = int(name == "p1b")
                                last = nc.scalar.activation(gelu[:, c, :], src, ACT.Gelu, bias=b_p1[:, c:c + 1])
                            elif name in ("ql", "qs", "p2", "mo"):
                                if name == "ql" and not first(n):
                                    act.wait_ge(tiles_st, 16 * n)
                                slot = {"ql": T_QL, "qs": T_QS, "p2": T_PRED, "mo": T_MEM}[name]
                                dst = tiles_out[:, :, slot, :]
                                src = src.rearrange("p (t n) -> p t n", n=P)
                                if name in ("p2", "mo"):
                                    bias = b_p2 if name == "p2" else b_mo
                                    last = nc.scalar.activation(dst, src, ACT.Identity, bias=bias[:, :])
                                else:
                                    last = nc.scalar.activation(dst, src, ACT.Copy)
                            elif name in ("kl", "ks"):
                                if name == "kl" and not first(n):
                                    act.wait_ge(kv_st, 32 * n)
                                last = nc.scalar.activation(kv_out[:, KV_SLOT[name], :], src, ACT.Copy)
                            elif name in ("v01", "v23"):
                                c = 2 * P * int(name == "v23")
                                last = nc.scalar.activation(
                                    kv_out[:, 2:4, c:c + 2 * P].rearrange("p h (t n) -> p t h n", n=P),
                                    src.rearrange("p (t h n) -> p t h n", t=2, h=2), ACT.Copy)
                            else:
                                k = int(name[2])
                                if k == 0:
                                    act.wait_ge(xnT_st, 16 * (n + 1))
                                    act.wait_ge(xlo_ready, KT * (n + 1))
                                nc.scalar.activation(xnT[:, k, :], src, ACT.Copy)
                                last = nc.scalar.activation(xnT_hi[:, 1 - hh, k, :], src, ACT.Copy)
                            last.then_inc(bank_read, 1)

                steps(0)
                with act.Fori(1, B) as b:
                    steps(b)

            @block.vector
            def _(dve):
                def subtract(out, value, hi):
                    return nc.vector.tensor_tensor(out, value, hi.bitcast(F32), ALU.subtract)

                def layer_norm(n):
                    if not first(n):
                        nc.vector.sem_clear(ln_step)
                    dve.wait_ge(x_in, 16 * (n + 1))
                    step = [0]

                    def link(ins):
                        ins.then_inc(ln_step, 1)
                        step[0] = step[0] + 1
                        dve.wait_ge(ln_step, step[0])

                    for t in range(HTILES):
                        last = nc.vector.bn_stats(stats[:, t, :], xin[:, t, :])
                    link(last)
                    for t in range(HTILES):
                        last = nc.vector.bn_aggr(mv[:, t, :], stats[:, t, :])
                    link(last)
                    link(nc.vector.tensor_scalar(var[:, :], mv[:, :, 1], EPS, None, ALU.add))
                    link(nc.vector.tensor_scalar(rstd[:, :].bitcast(I32), var[:, :].bitcast(I32),
                                                 -0.5, RSQRT_SEED, ALU.mult, ALU.add))
                    link(nc.vector.tensor_scalar(var[:, :], var[:, :], -0.5, None, ALU.mult))
                    for _ in range(NEWTON):
                        link(nc.vector.tensor_tensor(nt[:, :], rstd[:, :], rstd[:, :], ALU.mult))
                        link(nc.vector.tensor_tensor(nt[:, :], nt[:, :], var[:, :], ALU.mult))
                        link(nc.vector.scalar_tensor_tensor(out=rstd[:, :], in0=nt[:, :], scalar=1.5, in1=rstd[:, :],
                                                            op0=ALU.add, op1=ALU.mult))
                    for t in range(HTILES):
                        last = nc.vector.tensor_scalar(xn[:, t, :], xin[:, t, :], mv[:, t, 0:1],
                                                       rstd[:, t:t + 1], ALU.subtract, ALU.mult)
                    last.then_inc(xn_ready, 1)

                layer_norm(0)
                dve.wait_ge(sm_in, 16 * SM_LOADS)
                dve.wait_ge(consts, CONSTS)
                nc.vector.tensor_copy(sm_hi[:, :, :], sm[:, :, :]).then_inc(sm_split, 1)
                dve.wait_ge(sm_split, 1)
                subtract(sm_lo[:, :, :], sm[:, :, :], sm_hi[:, :, :]).then_inc(sm_split, 1)
                for k in range(KT):
                    dve.wait_ge(bank_read, k + 1)
                    subtract(xnT_lo[:, 0, k, :], xnT[:, k, :], xnT_hi[:, 0, k, :]).then_inc(xlo_ready, 1)
                dve.wait_ge(bkT_out, 1)
                subtract(bkT_s[:, 1, :], bkT[:, :], bkT_s[:, 0, :]).then_inc(bkT_split, 1)
                dve.wait_ge(rows_in, 16 * 3)
                dve.wait_ge(consts, CONSTS)
                nc.vector.tensor_copy(pick[:, :], pick32[:, :])
                nc.vector.tensor_scalar(half_bias[:, :], half_bias[:, :], 0.5, None, ALU.mult)
                nc.vector.tensor_copy(rows[:, :], rows32[:, :]).then_inc(rows_h, 1)
                dve.wait_ge(rows_h, 1)
                lo_rows = slice(LO_ROW, 2 * LO_ROW)
                subtract(rows[lo_rows, :], rows32[lo_rows, :], rows[lo_rows, :])
                layer_norm(1)

                def steps(b):
                    for hh in range(2):
                        n = 2 * b + hh
                        for name, slot in (("mp", XP), ("pi", PIN)):
                            dve.wait_ge(bank_read, done(n, name))
                            subtract(act_lo[:, slot, :], act32[:, slot, :], act_hi[:, slot, :]).then_inc(lo_ready, 1)
                        dve.wait_ge(job_done, done(n, "ms"))
                        part = ps[:, bank(hh, "ms"), :].rearrange("p (t i m) -> p t i m", i=2, m=MEM)
                        nc.vector.tensor_copy(mscore[:, :, :], part[:, :, 1, :]).then_inc(ms_step, 1)
                        dve.wait_ge(ms_step, 2 * n + 1)
                        nc.vector.tensor_tensor(mscore[:, :, :], mscore[:, :, :], part[:, :, 0, :], ALU.add)\
                            .then_inc(ms_step, 1)
                        dve.wait_ge(ms_step, 2 * n + 2)
                        nc.vector.tensor_reduce(nmx[:, :], mscore[:, :, :], AX_X, ALU.max,
                                                negate=True).then_inc(max_ready, 1)
                        dve.wait_ge(bank_read, done(n, "ms"))
                        nc.vector.reciprocal(einv[:, :], esum[:, :]).then_inc(inv_ready, 1)
                        dve.wait_ge(inv_ready, n + 1)
                        for t in range(HTILES):
                            last = nc.vector.tensor_scalar(we[:, t, :], we[:, t, :], einv[:, t:t + 1], None, ALU.mult)
                        last.then_inc(wn_ready, 1)
                        dve.wait_ge(bank_read, done(n, "p1b"))
                        nc.vector.tensor_copy(gelu_hi[:, :, :], gelu[:, :, :]).then_inc(ghi_ready, 1)
                        dve.wait_ge(bank_read, done(n, "wt"))
                        subtract(act_lo[0:MEM, WT, :], act32[0:MEM, WT % 2, :], act_hi[0:MEM, WT, :]).then_inc(lo_ready, 1)
                        dve.wait_ge(ghi_ready, n + 1)
                        subtract(gelu_lo[:, :, :], gelu[:, :, :], gelu_hi[:, :, :]).then_inc(lo_ready, 1)
                        dve.wait_ge(bank_read, done(n, "ret"))
                        subtract(act_lo[:, RET, :], act32[:, RET % 2, :], act_hi[:, RET, :]).then_inc(lo_ready, 1)
                        for k in range(KT):
                            dve.wait_ge(bank_read, done(n, f"tr{k}"))
                            subtract(xnT_lo[:, 1 - hh, k, :], xnT[:, k, :], xnT_hi[:, 1 - hh, k, :])\
                                .then_inc(xlo_ready, 1)
                        layer_norm(n + 2)

                steps(0)
                with dve.Fori(1, B) as b:
                    steps(b)

            @block.tensor
            def _(pe):
                def transposes(k, bk):
                    for t in range(HTILES):
                        last = nc.tensor.transpose(ps[:, bk, t * P:(t + 1) * P], xn[:, t, k * P:(k + 1) * P],
                                                   ident[:, :])
                    return last

                pe.wait_ge(consts, CONSTS)
                pe.wait_ge(xn_ready, 1)
                for k in range(KT):
                    transposes(k, k).then_inc(job_done, 1)
                pe.wait_ge(sm_in, 16 * SM_LOADS)
                nc.tensor.transpose(ps[:, BANKS - 1, 0:MEM], sm[0:MEM, 6, :], ident[0:MEM, 0:MEM]).then_inc(bkT_ps, 1)

                def steps(b):
                    for hh in range(2):
                        n = 2 * b + hh
                        for name in JOBS:
                            bk = bank(hh, name)
                            dst = ps[:, bk, :]
                            free = bank_free(b, hh, name)
                            if free is not None:
                                pe.wait_ge(bank_read, free)
                            columns = {"mp": MP, "pi": PI, "ql": QL, "qs": QS, "kl": KL, "ks": KS}
                            if name in columns:
                                c = slice(columns[name] * P, (columns[name] + 1) * P)
                                for k in range(KT):
                                    if name == "mp":
                                        if first(n):
                                            pe.wait_ge(w_split, k + 1)
                                        pe.wait_ge(xlo_ready, KT * n + k + 1)
                                    last = product(nc, dst, wp_hi[:, k, c], wp_lo[:, k, c], xnT_hi[:, hh, k, :],
                                                   xnT_lo[:, hh, k, :], k == 0, k == KT - 1)
                            elif name == "ms":
                                pe.wait_ge(lo_ready, lo(n, "xp"))
                                if first(n):
                                    pe.wait_ge(bkT_split, 1)
                                for t in range(HTILES):
                                    c = slice(t * P, (t + 1) * P)
                                    nc.tensor.matmul(dst[:, 2 * t * MEM:2 * (t + 1) * MEM], act_hi[:, XP, c],
                                                     bkT_s[:, :, :], start=True, stop=False)
                                    last = nc.tensor.matmul(dst[:, 2 * t * MEM:(2 * t + 1) * MEM], act_lo[:, XP, c],
                                                            bkT_s[:, 0, :], start=False, stop=True)
                            elif name in ("p1a", "p1b"):
                                c = 2 + int(name == "p1b")
                                pe.wait_ge(lo_ready, lo(n, "pin"))
                                if first(n):
                                    pe.wait_ge(sm_split, 2)
                                last = product(nc, dst, sm_hi[:, c, :], sm_lo[:, c, :], act_hi[:, PIN, :],
                                               act_lo[:, PIN, :], True, True)
                            elif name == "wt":
                                wait_alone(pe, wn_ready, n + 1, pe_passed)
                                for t in range(HTILES):
                                    last = nc.tensor.transpose(ps[0:MEM, bk, t * P:(t + 1) * P], we[:, t, :],
                                                               ident[:, :])
                            elif name == "ret":
                                pe.wait_ge(lo_ready, lo(n, "wt"))
                                last = product(nc, dst, sm_hi[0:MEM, 6, :], sm_lo[0:MEM, 6, :],
                                               act_hi[0:MEM, WT, :], act_lo[0:MEM, WT, :], True, True)
                            elif name == "p2":
                                pe.wait_ge(lo_ready, lo(n, "gelu"))
                                for c in range(2):
                                    last = product(nc, dst, sm_hi[:, 4 + c, :], sm_lo[:, 4 + c, :],
                                                   gelu_hi[:, c, :], gelu_lo[:, c, :], c == 0, c == 1)
                            elif name == "mo":
                                pe.wait_ge(lo_ready, lo(n, "ret"))
                                for c, slot in enumerate((XP, RET)):
                                    last = product(nc, dst, sm_hi[:, c, :], sm_lo[:, c, :], act_hi[:, slot, :],
                                                   act_lo[:, slot, :], c == 0, c == 1)
                            elif name in ("v01", "v23"):
                                v = slice(VL * P, (VS + 1) * P)
                                for tt in range(2):
                                    t = 2 * int(name == "v23") + tt
                                    c = slice(t * P, (t + 1) * P)
                                    for k in range(KT):
                                        last = product(nc, dst[:, tt * 2 * P:(tt + 1) * 2 * P], xnT_hi[:, hh, k, c],
                                                       xnT_lo[:, hh, k, c], wp_hi[:, k, v], wp_lo[:, k, v],
                                                       k == 0, k == KT - 1)
                            else:
                                if name == "tr0":
                                    pe.wait_ge(xn_ready, n + 2)
                                last = transposes(int(name[2]), bk)
                            last.then_inc(job_done, 1)

                steps(0)
                with pe.Fori(1, B) as b:
                    steps(b)


def stage2(nc, x, w, xnT_d, kv_d, tile_d, ident, ww_hi, ww_lo, rows, pick, half_bias, w2, b1, out):
    HC = CH // HTILES
    BC = 2 * CH

    with ExitStack() as ctx:
        def sb(name, shape, dt):
            return ctx.enter_context(nc.sbuf_tensor(name, shape, dt))

        def sem(name):
            return ctx.enter_context(nc.semaphore(name))

        units = sb("units", [P, 4, HALF], F32)
        xnT_hi = sb("xnT_hi", [P, KT, HALF], F32R)
        xnT_lo = sb("xnT_lo", [P, KT, HALF], F32R)
        kv_hi = sb("kv_hi", [P, 8, HALF], F32R)
        kv_lo = sb("kv_lo", [P, 8, HALF], F32R)
        tl = sb("tl", [P, 4, P], F32)
        tl_hi = sb("tl_hi", [P, 2, 4, P], F32R)
        tl_lo = sb("tl_lo", [P, 2, 4, P], F32R)
        w1 = sb("w1", [P, 2, KT, P], F32)
        w1_hi = sb("w1_hi", [P, 2, KT, P], F32R)
        w1_lo = sb("w1_lo", [P, 2, KT, P], F32R)
        w2_hi = sb("w2_hi", [P, 2, D], F32R)
        w2_lo = sb("w2_lo", [P, 2, D], F32R)
        h32 = sb("h32", [P, 2, HALF], F32)
        h_hi = sb("h_hi", [P, 2, HALF], F32R)
        h_lo = sb("h_lo", [P, 2, HALF], F32R)
        sc = sb("sc", [P, 2, S], F32)
        larger = sb("larger", [P, S // 2], F32)
        smaller = sb("smaller", [P, S // 2], F32)
        top_l = sb("top_l", [P, 8 * ROUNDS], F32)
        top_s = sb("top_s", [P, 1 + 8 * ROUNDS_S], F32)
        ranked = sb("ranked", [P, 1 + 8 * ROUNDS_S], F32)
        kth = sb("kth", [P, 1], F32)
        nms = sb("nms", [P, 2], F32)
        mxl = sb("mxl", [P, 1], F32)
        nml = sb("nml", [P, 1], F32)
        sums = sb("sums", [P, 2], F32)
        inv = sb("inv", [P, 2], F32)
        prob = sb("prob", [P, 2, S], F32)
        pT = sb("pT", [P, 2, 512], F32)
        pT_s = sb("pT_s", [P, TILES, 2, P], F32R)
        at = sb("at", [P, 2, 2, P], F32)
        at_hi = sb("at_hi", [P, 2, P], F32R)
        at_lo = sb("at_lo", [P, 2, P], F32R)
        mixed = sb("mixed", [P, HTILES, D], F32)
        gate = sb("gate", [P, HTILES, D], F32)
        xin = sb("xin", [P, D], F32)
        scores = ctx.enter_context(nc.psum_tensor("scores", [P, S], F32))
        hid = ctx.enter_context(nc.psum_tensor("hid", [P, HALF], F32))
        o = ctx.enter_context(nc.psum_tensor("o", [P, D], F32))
        acc = ctx.enter_context(nc.psum_tensor("acc", [P, HTILES, D], F32))

        w1_in = [sem("w1_in0"), sem("w1_in1")]
        units_in = [sem(f"units_in{j}") for j in range(4)]
        xr_in = sem("xr_in")
        tl_in = sem("tl_in")
        out_st = [sem(f"out_st{t}") for t in range(HTILES)]
        w1_h, w1_l = sem("w1_h"), sem("w1_l")
        w2_h, w2_l = sem("w2_h"), sem("w2_l")
        kv_h, kv_l = sem("kv_h"), sem("kv_l")
        xn_h, xn_l = sem("xn_h"), sem("xn_l")
        tl_h, tl_l = sem("tl_h"), sem("tl_l")
        h_h, h_l = sem("h_h"), sem("h_l")
        pT_h, pT_l = sem("pT_h"), sem("pT_l")
        at_h, at_l = sem("at_h"), sem("at_l")
        f1_done = sem("f1_done")
        f2_done = sem("f2_done")
        ffn_done = sem("ffn_done")
        ss_done = sem("ss_done")
        sl_done = sem("sl_done")
        tr_done = sem("tr_done")
        pv_done = sem("pv_done")
        mix_done = sem("mix_done")
        sc_ready = sem("sc_ready")
        tanh_ready = sem("tanh_ready")
        es_ready = sem("es_ready")
        el_ready = sem("el_ready")
        pr_ready = sem("pr_ready")
        step = sem("step")
        nms_ready = sem("nms_ready")
        nml_step = sem("nml_step")
        nml_ready = sem("nml_ready")
        masked = sem("masked")
        invs_ready = sem("invs_ready")
        invl_ready = sem("invl_ready")
        gate_ready = sem("gate_ready")
        mix_ready = sem("mix_ready")
        at_left = sem("at_left")
        prod_ready = sem("prod_ready")
        fin_ready = sem("fin_ready")

        sp_passed, dve_passed = sem("sp_passed"), sem("dve_passed")

        R_GATES, R_MAX, R_INVERSE, R_MIX = 2, 4, 5, 10
        STEPS = 2 + (2 * ROUNDS - 1) + (2 * ROUNDS_S - 1) + 2

        def known_first(v, least):
            return isinstance(v, int) and v < least

        with nc.Block() as block:
            @block.sync
            def _(sp):
                def load_w1(C, c):
                    if not known_first(C, 2):
                        sp.wait_ge(w1_l, C - 1)
                    sp.dma_start(w1[:, c % 2, :, :], w["w1"].rearrange("(k p) n -> p k n", p=P)
                                 [:, :, (c % CH) * P:(c % CH + 1) * P]).then_inc(w1_in[c % 2], 16)

                def load_kv(b, u, src):
                    before = 8 * b + u - 3
                    if not known_first(before, 1):
                        wait_alone(sp, xn_l, before, sp_passed)
                    sp.dma_start(units[:, u % 4, :], kv_d[bass.ds(src, 1), :, u, :]
                                 .rearrange("a p n -> p (a n)")).then_inc(units_in[u % 4], 16)

                def load_xn(h, k, src):
                    wait_alone(sp, kv_l, 4 * h + k + 1, sp_passed)
                    sp.dma_start(units[:, k, :], xnT_d[bass.ds(src, 1), :, k, :]
                                 .rearrange("a p n -> p (a n)")).then_inc(units_in[k], 16)

                def load_tl(m, src):
                    if not known_first(m, 1):
                        wait_alone(sp, tl_l, m, sp_passed)
                    sp.dma_start(tl[:, :, :], tile_d[bass.ds(src, 1), :, :, :]
                                 .rearrange("a p s n -> p (a s) n")).then_inc(tl_in, 16)

                load_tl(0, 0)
                load_kv(0, U_KS, 0)
                load_kv(0, U_KS + 1, 0)
                load_w1(0, 0)
                load_kv(0, U_KL, 0)
                load_kv(0, U_KL + 1, 0)
                load_w1(1, 1)
                for k in range(KT):
                    load_xn(0, k, 0)
                load_w1(2, 2)
                load_w1(3, 3)
                for u in range(4, 8):
                    load_kv(0, u, 0)

                def load_x(m, b, T):
                    if not known_first(m, 1):
                        wait_alone(sp, fin_ready, m, sp_passed)
                    sp.dma_start(xin[:, :], x[bass.ds(b, 1), T * P:(T + 1) * P, :]
                                 .rearrange("a p n -> p (a n)")).then_inc(xr_in, 16)

                def store(m, b, T):
                    wait_alone(sp, fin_ready, m + 1, sp_passed)
                    sp.dma_start(out[bass.ds(b, 1), T * P:(T + 1) * P, :].rearrange("a p n -> p (a n)"),
                                 gate[:, T % HTILES, :]).then_inc(out_st[T % HTILES], 16)

                def slots(b):
                    nb = (b + 1) & (B - 1)
                    for T in range(TILES):
                        m, C = b * TILES + T, b * BC + T * HC
                        load_w1(C + 4, T * HC + 4)
                        load_tl(m + 1, m + 1 if T < TILES - 1 else nb * TILES)
                        if T == 1:
                            load_xn(2 * b + 1, 2, 2 * b + 1)
                            load_xn(2 * b + 1, 3, 2 * b + 1)
                        if T == TILES - 1:
                            load_xn(2 * b + 2, 0, 2 * nb)
                            load_xn(2 * b + 2, 1, 2 * nb)
                        load_w1(C + 5, T * HC + 5)
                        if T == 0:
                            load_xn(2 * b + 1, 0, 2 * b + 1)
                            load_xn(2 * b + 1, 1, 2 * b + 1)
                        if not known_first(m, HTILES):
                            store(m - 4, b if T >= 4 else b - 1, (T - 4) % TILES)
                        if not known_first(m, HTILES - 1):
                            load_x(m - 3, b if T >= 3 else b - 1, (T - 3) % TILES)
                        load_w1(C + 6, T * HC + 6)
                        if T == TILES - 1:
                            load_xn(2 * b + 2, 2, 2 * nb)
                            load_xn(2 * b + 2, 3, 2 * nb)
                        if T % HTILES == HTILES - 1:
                            for u in range(4):
                                load_kv(b + 1, u + (0 if T < HTILES else 4), nb)
                        load_w1(C + 7, T * HC + 7)

                slots(0)
                with sp.Fori(1, B) as b:
                    slots(b)
                for T in range(HTILES, TILES):
                    m = (B - 1) * TILES + T
                    store(m, B - 1, T)
                    if T < TILES - 1:
                        load_x(m + 1, B - 1, T + 1)
                for t in range(HTILES):
                    sp.wait_ge(out_st[t], 16 * 2 * B)
                for j in range(2):
                    sp.wait_ge(w1_in[j], 16 * (B * BC // 2 + 2))

            @block.scalar
            def _(act):
                def hi(out_, src, ready):
                    return nc.scalar.activation(out_, src, ACT.Copy).then_inc(ready, 1)

                def split_w1(C, c):
                    act.wait_ge(w1_in[c % 2], 8 * (C - c % 2) + 16)
                    hi(w1_hi[:, c % 2, :, :], w1[:, c % 2, :, :], w1_h)

                def split_kv(b, u):
                    act.wait_ge(units_in[u % 4], 64 * b + 8 * (u - u % 4) + 16)
                    hi(kv_hi[:, u, :], units[:, u % 4, :], kv_h)

                def split_xn(h, k):
                    act.wait_ge(units_in[k], 32 * h + 32)
                    hi(xnT_hi[:, k, :], units[:, k, :], xn_h)

                def split_tl(m, parity):
                    act.wait_ge(tl_in, 16 * m + 16)
                    hi(tl_hi[:, parity, :, :], tl[:, :, :], tl_h)

                def sparse_scores(m, parity):
                    act.wait_ge(ss_done, m + 1)
                    if not known_first(m, 2):
                        act.wait_ge(masked, m - 1)
                    nc.scalar.activation(sc[:, parity, :], scores[:, :], ACT.Copy, scale=SCALE).then_inc(sc_ready, 1)

                def chunk(C, c, h_next):
                    act.wait_ge(f1_done, C + 1)
                    if not known_first(C, 2):
                        act.wait_ge(h_l, C - 1)
                        act.wait_ge(f2_done, C - 1)
                    bias = b1[:, c % CH:c % CH + 1]
                    nc.scalar.activation(h32[:, c % 2, :], hid[:, :], ACT.Relu, bias=bias)
                    nc.scalar.activation(h_hi[:, c % 2, :], hid[:, :], ACT.Relu, bias=bias).then_inc(h_h, 1)
                    hi(w2_hi[:, c % 2, :], w2[:, c % CH, :], w2_h)
                    if c % CH == CH - 1:
                        for k in range(KT):
                            split_xn(h_next, k)
                    split_w1(C + 2, c + 2)

                def transposed(i):
                    act.wait_ge(tr_done, i + 1)
                    for j in range(2):
                        if not known_first(i, 1):
                            act.wait_ge(pT_l, 2 * i - 1 + j)
                        c = slice(j * 512, (j + 1) * 512)
                        nc.scalar.activation(pT[:, j, :], scores[:, c], ACT.Copy)
                        nc.scalar.activation(pT_s[:, j * HTILES:(j + 1) * HTILES, 0, :],
                                             scores[:, c].rearrange("p (t n) -> p t n", n=P), ACT.Copy)\
                            .then_inc(pT_h, 1)

                def head_out(i, head):
                    act.wait_ge(pv_done, i + 1)
                    nc.scalar.activation(at[:, head, :, :], o[:, 0:2 * P].rearrange("p (i n) -> p i n", n=P), ACT.Copy)
                    nc.scalar.activation(at_hi[:, head, :], o[:, 0:P], ACT.Copy).then_inc(at_h, 1)

                def gates(h):
                    for t in range(HTILES):
                        act.wait_ge(ffn_done, HTILES * h + t + 1)
                        if not known_first(h, 1):
                            act.wait_ge(out_st[t], 16 * h)
                        nc.scalar.activation(gate[:, t, :], acc[:, t, :], ACT.Tanh, scale=0.5).then_inc(tanh_ready, 1)

                split_tl(0, 0)
                split_kv(0, U_KS)
                split_kv(0, U_KS + 1)
                split_w1(0, 0)
                split_kv(0, U_KL)
                split_kv(0, U_KL + 1)
                split_w1(1, 1)
                for k in range(KT):
                    split_xn(0, k)

                def sparse_probabilities(m):
                    act.wait_ge(invs_ready, m + 1)
                    nc.scalar.activation(prob[:, 1, :], prob[:, 1, :], ACT.Copy, scale=inv[:, 1:2]).then_inc(pr_ready, 1)

                def slots(b):
                    for T in range(TILES):
                        m, C, c = b * TILES + T, b * BC + T * HC, T * HC
                        h = 2 * b + T // HTILES
                        some = not known_first(m, 1)
                        sparse_scores(m, T % 2)
                        chunk(C, c, h + 1)
                        if some:
                            head_out(2 * m - 2, 0)
                        if some:
                            sparse_probabilities(m - 1)
                        if T % HTILES == 0 and some:
                            gates(h - 1)
                        if some:
                            transposed(2 * m - 1)
                        if T == 1:
                            split_kv(b, U_VS)
                            split_kv(b, U_VS + 1)
                        if T == TILES - 1:
                            split_kv(b + 1, U_KS)
                            split_kv(b + 1, U_KS + 1)
                        chunk(C + 1, c + 1, h + 1)
                        act.wait_ge(nms_ready, m + 1)
                        nc.scalar.activation(prob[:, 1, :], sc[:, T % 2, :], ACT.Exp, bias=nms[:, T % 2:T % 2 + 1])\
                            .then_inc(es_ready, 1)
                        if T == 0:
                            split_kv(b, U_VL)
                            split_kv(b, U_VL + 1)
                        if some:
                            head_out(2 * m - 1, 1)
                        act.wait_ge(nml_ready, m + 1)
                        nc.scalar.activation(prob[:, 0, :], scores[:, :], ACT.Exp, bias=nml[:, :], scale=SCALE,
                                             accum_out=sums[:, 0:1]).then_inc(el_ready, 1)
                        act.wait_ge(invl_ready, m + 1)
                        nc.scalar.activation(prob[:, 0, :], prob[:, 0, :], ACT.Copy, scale=inv[:, 0:1])\
                            .then_inc(pr_ready, 1)
                        chunk(C + 2, c + 2, h + 1)
                        if T == TILES - 1:
                            split_kv(b + 1, U_KL)
                            split_kv(b + 1, U_KL + 1)
                        if some:
                            act.wait_ge(mix_done, m)
                        split_tl(m + 1, (T + 1) % 2)
                        transposed(2 * m)
                        chunk(C + 3, c + 3, h + 1)

                slots(0)
                with act.Fori(1, B) as b:
                    slots(b)
                head_out(2 * B * TILES - 2, 0)
                sparse_probabilities(B * TILES - 1)
                gates(2 * B - 1)
                transposed(2 * B * TILES - 1)
                head_out(2 * B * TILES - 1, 1)

            @block.gpsimd
            def _(pool):
                def lo(out_, value, hi_, ready):
                    return nc.gpsimd.tensor_tensor(out_, value, hi_.bitcast(F32), ALU.subtract).then_inc(ready, 1)

                def split_w1(C, c):
                    pool.wait_ge(w1_h, C + 1)
                    lo(w1_lo[:, c % 2, :, :], w1[:, c % 2, :, :], w1_hi[:, c % 2, :, :], w1_l)

                def split_kv(b, u):
                    pool.wait_ge(kv_h, 8 * b + u + 1)
                    lo(kv_lo[:, u, :], units[:, u % 4, :], kv_hi[:, u, :], kv_l)

                def split_tl(m, parity):
                    pool.wait_ge(tl_h, m + 1)
                    lo(tl_lo[:, parity, :, :], tl[:, :, :], tl_hi[:, parity, :, :], tl_l)

                def chunk(C, c):
                    pool.wait_ge(h_h, C + 1)
                    lo(h_lo[:, c % 2, :], h32[:, c % 2, :], h_hi[:, c % 2, :], h_l)
                    pool.wait_ge(w2_h, C + 1)
                    lo(w2_lo[:, c % 2, :], w2[:, c % CH, :], w2_hi[:, c % 2, :], w2_l)
                    split_w1(C + 2, c + 2)

                def transposed(i):
                    for j in range(2):
                        pool.wait_ge(pT_h, 2 * i + j + 1)
                        half = slice(j * HTILES, (j + 1) * HTILES)
                        lo(pT_s[:, half, 1, :], pT[:, j, :].rearrange("p (t n) -> p t n", n=P), pT_s[:, half, 0, :], pT_l)

                def head_out(i, head):
                    pool.wait_ge(at_h, i + 1)
                    lo(at[:, head, 0, :], at[:, head, 0, :], at_hi[:, head, :], at_left)
                    pool.wait_ge(at_left, i + 1)
                    nc.gpsimd.tensor_tensor(at_lo[:, head, :], at[:, head, 0, :], at[:, head, 1, :], ALU.add)\
                        .then_inc(at_l, 1)

                def residual(m, T):
                    t = T % HTILES
                    pool.wait_ge(gate_ready, m + 1)
                    pool.wait_ge(mix_ready, m + 1)
                    nc.gpsimd.tensor_tensor(gate[:, t, :], gate[:, t, :], mixed[:, t, :], ALU.mult)\
                        .then_inc(prod_ready, 1)
                    pool.wait_ge(prod_ready, m + 1)
                    pool.wait_ge(xr_in, 16 * m + 16)
                    nc.gpsimd.tensor_tensor(gate[:, t, :], gate[:, t, :], xin[:, :], ALU.add)\
                        .then_inc(fin_ready, 1)

                split_tl(0, 0)
                split_kv(0, U_KS)
                split_kv(0, U_KS + 1)
                split_w1(0, 0)
                split_kv(0, U_KL)
                split_kv(0, U_KL + 1)
                split_w1(1, 1)

                def slots(b):
                    for T in range(TILES):
                        m, C, c = b * TILES + T, b * BC + T * HC, T * HC
                        some = not known_first(m, 1)
                        chunk(C, c)
                        if some:
                            head_out(2 * m - 2, 0)
                        if some:
                            transposed(2 * m - 1)
                        if T == 1:
                            split_kv(b, U_VS)
                            split_kv(b, U_VS + 1)
                        if T == TILES - 1:
                            split_kv(b + 1, U_KS)
                            split_kv(b + 1, U_KS + 1)
                        chunk(C + 1, c + 1)
                        if T == 0:
                            split_kv(b, U_VL)
                            split_kv(b, U_VL + 1)
                        if some:
                            head_out(2 * m - 1, 1)
                        if not known_first(m, HTILES):
                            residual(m - HTILES, T)
                        chunk(C + 2, c + 2)
                        if T == TILES - 1:
                            split_kv(b + 1, U_KL)
                            split_kv(b + 1, U_KL + 1)
                        split_tl(m + 1, (T + 1) % 2)
                        transposed(2 * m)
                        chunk(C + 3, c + 3)

                slots(0)
                with pool.Fori(1, B) as b:
                    slots(b)
                head_out(2 * B * TILES - 2, 0)
                last = (B - 1) * TILES
                residual(last + HTILES, HTILES)
                transposed(2 * B * TILES - 1)
                residual(last + HTILES + 1, HTILES + 1)
                head_out(2 * B * TILES - 1, 1)
                for T in range(HTILES + 2, TILES):
                    residual(last + T, T)

            @block.vector
            def _(dve):
                def apply_threshold(m, T):
                    dve.wait_ge(step, 1 + STEPS * (T + 1))
                    dve.wait_ge(es_ready, m + 1)
                    nc.vector.scalar_tensor_tensor(out=prob[:, 1, :], in0=sc[:, T % 2, :], scalar=kth[:, :],
                                                   in1=prob[:, 1, :], op0=ALU.is_ge, op1=ALU.mult,
                                                   accum_out=sums[:, 1:2]).then_inc(masked, 1)
                    dve.wait_ge(masked, m + 1)
                    nc.vector.reciprocal(inv[:, 1:2], sums[:, 1:2]).then_inc(invs_ready, 1)

                def gates(h):
                    for t in range(HTILES):
                        dve.wait_ge(tanh_ready, HTILES * h + t + 1)
                        nc.vector.scalar_tensor_tensor(out=gate[:, t, :], in0=gate[:, t, :], scalar=1.0,
                                                       in1=acc[:, t, :], op0=ALU.add, op1=ALU.mult)\
                            .then_inc(gate_ready, 1)

                def mix(m, t):
                    dve.wait_ge(mix_done, m + 1)
                    if not known_first(m, HTILES):
                        dve.wait_ge(prod_ready, m - HTILES + 1)
                    nc.vector.scalar_tensor_tensor(out=mixed[:, t, :], in0=o[:, :], scalar=0.5, in1=half_bias[:, :],
                                                   op0=ALU.mult, op1=ALU.add).then_inc(mix_ready, 1)

                def full_max(m):
                    dve.wait_ge(sl_done, m + 1)
                    nc.vector.tensor_reduce(mxl[:, :], scores[:, :], AX_X, ALU.max).then_inc(nml_step, 1)
                    dve.wait_ge(nml_step, m + 1)
                    nc.vector.tensor_scalar(nml[:, :], mxl[:, :], -SCALE, None, ALU.mult).then_inc(nml_ready, 1)

                def full_inverse(m):
                    dve.wait_ge(el_ready, m + 1)
                    nc.vector.reciprocal(inv[:, 0:1], sums[:, 0:1]).then_inc(invl_ready, 1)

                def search(m, T, b):
                    done = [1 + STEPS * T]
                    r_max, r_inverse = (3, 4) if known_first(m, 1) else (R_MAX, R_INVERSE)

                    def count(ins):
                        ins.then_inc(step, 1)
                        done[0] += 1
                        return done[0]

                    wait_alone(dve, sc_ready, m + 1, dve_passed)
                    lo_half, hi_half = sc[:, T % 2, 0:S // 2], sc[:, T % 2, S // 2:S]
                    l_step = count(nc.vector.tensor_tensor(larger[:, :], lo_half, hi_half, ALU.max))
                    s_step = count(nc.vector.tensor_tensor(smaller[:, :], lo_half, hi_half, ALU.min))
                    for r in range(ROUNDS):
                        own = slice(8 * r, 8 * r + 8)
                        dve.wait_ge(step, l_step)
                        l_step = count(nc.vector.max(top_l[:, own], larger[:, :]))
                        if r < ROUNDS_S:
                            own_s = slice(1 + 8 * r, 9 + 8 * r)
                            dve.wait_ge(step, s_step)
                            s_step = count(nc.vector.max(top_s[:, own_s], smaller[:, :]))
                        if r == R_MIX and not known_first(m, 1):
                            mix(m - 1, (T - 1) % HTILES)
                        if r == R_GATES:
                            gates_of_half(m, T, b)
                        if r == r_max:
                            full_max(m)
                        if r == r_inverse:
                            full_inverse(m)
                        if r < ROUNDS - 1:
                            dve.wait_ge(step, l_step)
                            l_step = count(nc.vector.match_replace(larger[:, :], top_l[:, own], larger[:, :], LOWEST))
                        if r < ROUNDS_S - 1:
                            dve.wait_ge(step, s_step)
                            s_step = count(nc.vector.match_replace(smaller[:, :], top_s[:, own_s], smaller[:, :],
                                                                   LOWEST))
                        if r == 0:
                            nc.vector.tensor_scalar(nms[:, T % 2:T % 2 + 1], top_l[:, 0:1], -1.0, None, ALU.mult)\
                                .then_inc(nms_ready, 1)
                    n = 1 + 8 * ROUNDS_S
                    dve.wait_ge(step, l_step)
                    merged = count(nc.vector.tensor_tensor(ranked[:, :], top_l[:, TOPK - n:TOPK], top_s[:, ::-1],
                                                           ALU.min))
                    dve.wait_ge(step, merged)
                    count(nc.vector.tensor_reduce(kth[:, :], ranked[:, :], AX_X, ALU.max))
                    assert done[0] == 1 + STEPS * (T + 1)

                def gates_of_half(m, T, b):
                    if T % HTILES == 0 and not known_first(m, 1):
                        gates(2 * b + T // HTILES - 1)

                def split_xn(h):
                    for k in range(KT):
                        dve.wait_ge(xn_h, KT * h + k + 1)
                        nc.vector.tensor_tensor(xnT_lo[:, k, :], units[:, k, :], xnT_hi[:, k, :].bitcast(F32),
                                                ALU.subtract).then_inc(xn_l, 1)

                split_xn(0)

                def slots(b):
                    for T in range(TILES):
                        m = b * TILES + T
                        if not known_first(m, 1):
                            apply_threshold(m - 1, (T - 1) % TILES)
                        if T == 0:
                            if not known_first(m, 1):
                                nc.vector.sem_clear(step)
                            nc.vector.memset(top_s[:, 0:1], HIGHEST).then_inc(step, 1)
                            dve.wait_ge(step, 1)
                        search(m, T, b)
                        if T % HTILES == HTILES - 1:
                            split_xn(2 * b + 1 + T // HTILES)

                slots(0)
                with dve.Fori(1, B) as b:
                    slots(b)
                apply_threshold(B * TILES - 1, TILES - 1)
                gates(2 * B - 1)
                mix(B * TILES - 1, HTILES - 1)

            @block.tensor
            def _(pe):
                def f1(C, c, h):
                    pe.wait_ge(w1_l, C + 1)
                    if not known_first(C, 1):
                        pe.wait_ge(h_h, C)
                    for k in range(KT):
                        if c % CH == 0:
                            pe.wait_ge(xn_l, KT * h + k + 1)
                        last = product(nc, hid[:, :], w1_hi[:, c % 2, k, :], w1_lo[:, c % 2, k, :],
                                       xnT_hi[:, k, :], xnT_lo[:, k, :], k == 0, k == KT - 1)
                    last.then_inc(f1_done, 1)

                def f2(C, c, h):
                    pe.wait_ge(h_l, C + 1)
                    pe.wait_ge(w2_l, C + 1)
                    start = c % CH == 0
                    for t in range(HTILES):
                        if start and not known_first(C, 1):
                            pe.wait_ge(gate_ready, HTILES * (h - 1) + t + 1)
                        last = product(nc, acc[:, t, :], h_hi[:, c % 2, t * P:(t + 1) * P],
                                       h_lo[:, c % 2, t * P:(t + 1) * P], w2_hi[:, c % 2, :], w2_lo[:, c % 2, :],
                                       start, False)
                        if t == HTILES - 1:
                            last.then_inc(f2_done, 1)
                        if c % CH == CH - 1:
                            nc.tensor.matmul(acc[:, t, :], pick[:, :], rows[:, :], start=False, stop=True)\
                                .then_inc(ffn_done, 1)

                def head_scores(parity, slot, unit, done):
                    for j in range(2):
                        last = product(nc, scores[:, j * 512:(j + 1) * 512], tl_hi[:, parity, slot, :],
                                       tl_lo[:, parity, slot, :], kv_hi[:, unit + j, :], kv_lo[:, unit + j, :],
                                       True, True)
                    last.then_inc(done, 1)

                def transposes(i, head):
                    pe.wait_ge(pr_ready, i + 1)
                    for j in range(TILES):
                        last = nc.tensor.transpose(scores[:, j * P:(j + 1) * P], prob[:, head, j * P:(j + 1) * P],
                                                   ident[:, :])
                    last.then_inc(tr_done, 1)

                def head_out(i, unit):
                    for j in range(TILES):
                        if j % HTILES == 0:
                            pe.wait_ge(pT_l, 2 * i + 1 + j // HTILES)
                        u, c = unit + j // HTILES, slice((j % HTILES) * P, (j % HTILES + 1) * P)
                        if j == TILES - 1:
                            nc.tensor.matmul(o[:, 0:P], kv_lo[:, u, c], pT_s[:, j, 0, :], start=False, stop=False)
                        last = nc.tensor.matmul(o[:, 0:2 * P], kv_hi[:, u, c], pT_s[:, j, :, :], start=j == 0,
                                                stop=j == TILES - 1)
                        if j < TILES - 1:
                            nc.tensor.matmul(o[:, 0:P], kv_lo[:, u, c], pT_s[:, j, 0, :], start=False, stop=False)
                    last.then_inc(pv_done, 1)

                def sparse_head_out(m, b_kv):
                    pe.wait_ge(at_h, 2 * m + 1)
                    pe.wait_ge(kv_l, b_kv)
                    head_out(2 * m + 1, U_VS)

                def mix(m, parity):
                    pe.wait_ge(at_l, 2 * m + 2)
                    for j in range(2):
                        product(nc, o[:, :], at_hi[:, j, :], at_lo[:, j, :], ww_hi[:, j, :], ww_lo[:, j, :],
                                j == 0, False)
                    for j in (T_MEM, T_PRED):
                        last = product(nc, o[:, :], tl_hi[:, parity, j, :], tl_lo[:, parity, j, :], ww_hi[:, j, :],
                                       ww_lo[:, j, :], False, j == T_PRED)
                    last.then_inc(mix_done, 1)

                def sparse_scores(m, parity, kv_count):
                    pe.wait_ge(tl_l, m + 1)
                    if kv_count is not None:
                        pe.wait_ge(kv_l, kv_count)
                    head_scores(parity, T_QS, U_KS, ss_done)

                def slots(b):
                    for T in range(TILES):
                        m, C, c = b * TILES + T, b * BC + T * HC, T * HC
                        h, t = 2 * b + T // HTILES, T % HTILES
                        some = not known_first(m, 1)
                        if some:
                            pe.wait_ge(pT_h, 4 * m - 2)
                        sparse_scores(m, T % 2, 8 * b + U_KS + 2 if T == 0 else None)
                        f1(C, c, h)
                        if some:
                            if not known_first(m, 2):
                                pe.wait_ge(mix_ready, m - 1)
                            head_out(2 * m - 2, U_VL)
                        if some:
                            f2(C - 1, (c - 1) % BC, h if t > 0 else h - 1)
                        pe.wait_ge(sc_ready, m + 1)
                        if some:
                            transposes(2 * m - 1, 1)
                        f1(C + 1, c + 1, h)
                        if some:
                            pe.wait_ge(pT_h, 4 * m)
                        if T == 0:
                            pe.wait_ge(kv_l, 8 * b + U_KL + 2)
                        head_scores(T % 2, T_QL, U_KL, sl_done)
                        f2(C, c, h)
                        if some:
                            sparse_head_out(m - 1, 8 * b + (U_VS + 2 if T > 0 else 0))
                        f1(C + 2, c + 2, h)
                        f2(C + 1, c + 1, h)
                        if some:
                            mix(m - 1, (T + 1) % 2)
                        transposes(2 * m, 0)
                        f1(C + 3, c + 3, h)
                        f2(C + 2, c + 2, h)

                slots(0)
                with pe.Fori(1, B) as b:
                    slots(b)
                m = B * TILES - 1
                pe.wait_ge(mix_ready, m)
                head_out(2 * m, U_VL)
                f2(B * BC - 1, BC - 1, 2 * B - 1)
                pe.wait_ge(pT_h, 4 * m + 2)
                transposes(2 * m + 1, 1)
                sparse_head_out(m, 8 * B)
                mix(m, m % 2)


def program(nc, ins, out):
    names = {n.removeprefix("L0_attn_").removeprefix("L0_ffn_"): a for n, a in ins.items()}
    build(nc, names["x"], names, out)


_OUT = ((B, S, D), "float32")
_ORDER = ["L0_attn_x", "L0_attn_local_qkv_w", "L0_attn_sparse_qkv_w", "L0_attn_memory_bank",
          "L0_attn_memory_proj_w", "L0_attn_mem_out_w", "L0_attn_mem_out_b", "L0_attn_pred_in_w",
          "L0_attn_pred_in_b", "L0_attn_pred1_w", "L0_attn_pred1_b", "L0_attn_pred2_w", "L0_attn_pred2_b",
          "L0_attn_warboss_w", "L0_attn_warboss_b", "L0_ffn_w1", "L0_ffn_b1", "L0_ffn_w2", "L0_ffn_b2"]


def kernel(**inputs):
    import numpy as _np
    import concourse.bacc as _bacc
    from concourse import mybir as _mybir
    from concourse.bass_utils import run_bass_kernel_spmd as _run

    nc = _bacc.Bacc("TRN2", target_bir_lowering=False, num_devices=1)
    arrays, args = {}, {}
    for name in _ORDER:
        a = _np.ascontiguousarray(inputs[name])
        arrays[f"in_{name}"] = a
        args[name] = nc.dram_tensor(f"in_{name}", a.shape, _mybir.dt.from_np(a.dtype), kind="ExternalInput").ap()
    shape, dtype = _OUT
    out = nc.dram_tensor("out_0", shape, _mybir.dt.from_np(_np.dtype(dtype)), kind="ExternalOutput").ap()
    program(nc, args, out)
    r = _run(nc, [arrays], core_ids=[0])
    return r.results[0]["out_0"]
```
